# Optimizing a Trainium2 kernel written in Bass

```python
import numpy as np
import jax
import jax.numpy as jnp

def _softmax(x, axis=-1):
    return jax.nn.softmax(x, axis=axis)

def _gelu(x):
    return jax.nn.gelu(x, approximate=True)

def _silu(x):
    return jax.nn.silu(x)

def _sigmoid(x):
    return jax.nn.sigmoid(x)

def _layernorm(x, axis=-1, eps=1e-05):
    m = jnp.mean(x, axis=axis, keepdims=True)
    v = jnp.var(x, axis=axis, keepdims=True)
    return (x - m) / jnp.sqrt(v + eps)

def _scatter_add(tgt, idx, src, axis=0):
    return tgt.at[idx].add(src)

def _segment_sum(src, seg, n):
    return jax.ops.segment_sum(src, seg, n)
kernel_name = 'mk_hybrid_d2_jaxref_r8_187ce4'

def setup_inputs(seed: int=0):
    np.random.seed(seed)
    _w = jnp.asarray

    def _L0_attn_a_setup():
        import jax, jax.numpy as jnp
        import numpy as np
        import math
        INPUT_WIDTH = 128
        KEY_WIDTH = 64
        VALUE_WIDTH = 64
        NUM_HEADS = 16
        NUM_GROUPS = 4
        HEADS_PER_GROUP = NUM_HEADS // NUM_GROUPS
        key = jax.random.key(seed)
        k_x, k_q, k_k, k_v, k_p = jax.random.split(key, 5)
        n, s = (2, 256)

        def lin(k, fan_in, fan_out):
            bound = 1.0 / math.sqrt(fan_in)
            return jax.random.uniform(k, (fan_in, fan_out), minval=-bound, maxval=bound, dtype=jnp.float32)
        return {'X': jax.random.normal(k_x, (n, s, INPUT_WIDTH), dtype=jnp.float32), 'Wq': lin(k_q, INPUT_WIDTH, NUM_HEADS * KEY_WIDTH), 'Wk': lin(k_k, INPUT_WIDTH, NUM_GROUPS * KEY_WIDTH), 'Wv': lin(k_v, INPUT_WIDTH, NUM_GROUPS * VALUE_WIDTH), 'Wpost': lin(k_p, NUM_HEADS * VALUE_WIDTH, INPUT_WIDTH)}
    _L0_attn_a_in = _L0_attn_a_setup()

    def _L0_attn_b_setup():
        import jax, jax.numpy as jnp
        import numpy as np
        import math
        DIM = 128
        NUM_HEADS = 16
        HEAD_DIM = DIM // NUM_HEADS
        LAYER_IDX = 12
        LAMBDA_INIT = 0.8 - 0.6 * math.exp(-0.3 * (LAYER_IDX - 1))
        LN_EPS = 1e-05
        key = jax.random.key(seed)
        ks = jax.random.split(key, 11)
        B, S = (2, 256)
        x = jax.random.normal(ks[0], (B, S, DIM), dtype=jnp.float32)
        s = 1.0 / math.sqrt(DIM)
        Wq = jax.random.normal(ks[1], (DIM, 2 * DIM), dtype=jnp.float32) * s
        Wk = jax.random.normal(ks[2], (DIM, 2 * DIM), dtype=jnp.float32) * s
        Wv = jax.random.normal(ks[3], (DIM, DIM), dtype=jnp.float32) * s
        Wo = jax.random.normal(ks[4], (DIM, DIM), dtype=jnp.float32) * s
        lambda_q1 = jax.random.normal(ks[5], (HEAD_DIM,), dtype=jnp.float32) * 0.1
        lambda_k1 = jax.random.normal(ks[6], (HEAD_DIM,), dtype=jnp.float32) * 0.1
        lambda_q2 = jax.random.normal(ks[7], (HEAD_DIM,), dtype=jnp.float32) * 0.1
        lambda_k2 = jax.random.normal(ks[8], (HEAD_DIM,), dtype=jnp.float32) * 0.1
        gamma = jnp.ones((DIM,), dtype=jnp.float32)
        beta = jnp.zeros((DIM,), dtype=jnp.float32)
        return {'x': x, 'Wq': Wq, 'Wk': Wk, 'Wv': Wv, 'Wo': Wo, 'lambda_q1': lambda_q1, 'lambda_k1': lambda_k1, 'lambda_q2': lambda_q2, 'lambda_k2': lambda_k2, 'gamma': gamma, 'beta': beta}
    _L0_attn_b_in = _L0_attn_b_setup()

    def _L0_ffn_setup():
        import jax, jax.numpy as jnp
        import numpy as np
        DIM = 128

        def _reference_tuple_inner(x, W_r, W_k, W_v, mu_r, mu_k):
            B, T, C = x.shape
            x_prev = jnp.concatenate([jnp.zeros((B, 1, C), x.dtype), x[:, :-1, :]], axis=1)
            xr = mu_r * x + (1.0 - mu_r) * x_prev
            xk = mu_k * x + (1.0 - mu_k) * x_prev
            r = jax.nn.sigmoid(jnp.einsum('btc,dc->btd', xr, W_r))
            k = jnp.einsum('btc,dc->btd', xk, W_k)
            k_act = jnp.square(jax.nn.relu(k))
            out = r * jnp.einsum('btc,dc->btd', k_act, W_v)
            new_state = x[:, -1, :]
            return (out, new_state)
        key = jax.random.key(seed)
        ks = jax.random.split(key, 6)
        B, T, C = (8, 256, DIM)
        x = jax.random.normal(ks[0], (B, T, C), dtype=jnp.float32)
        s = 1.0 / np.sqrt(C)
        W_r = jax.random.uniform(ks[1], (C, C), jnp.float32, -s, s)
        W_k = jax.random.uniform(ks[2], (C, C), jnp.float32, -s, s)
        W_v = jax.random.uniform(ks[3], (C, C), jnp.float32, -s, s)
        mu_r = jax.random.uniform(ks[4], (C,), jnp.float32)
        mu_k = jax.random.uniform(ks[5], (C,), jnp.float32)
        return {'x': x, 'W_r': W_r, 'W_k': W_k, 'W_v': W_v, 'mu_r': mu_r, 'mu_k': mu_k}
    _L0_ffn_in = _L0_ffn_setup()

    def _L1_attn_a_setup():
        import jax, jax.numpy as jnp
        import numpy as np
        B, L, C, H = (8, 256, 128, 16)
        HID = 4 * C

        def _rope(x):
            b, n, c = x.shape
            k_max = c // 2
            theta = 1.0 / 10000.0 ** (jnp.arange(k_max, dtype=jnp.float32) / k_max)
            cos_t, sin_t = (jnp.cos(theta), jnp.sin(theta))
            xr = x.reshape(b, n, k_max, 2)
            re = xr[..., 0] * cos_t - xr[..., 1] * sin_t
            im = xr[..., 0] * sin_t + xr[..., 1] * cos_t
            return jnp.stack((re, im), axis=-1).reshape(b, n, c)

        def _dwconv(x_bcl, w, bias):
            y = jax.lax.conv_general_dilated(x_bcl, w, (1,), [(1, 1)], dimension_numbers=('NCH', 'OIH', 'NCH'), feature_group_count=x_bcl.shape[1])
            return y + bias[None, :, None]

        def _ln(x, g, b, eps=1e-05):
            mu = x.mean(-1, keepdims=True)
            var = ((x - mu) ** 2).mean(-1, keepdims=True)
            return (x - mu) * jax.lax.rsqrt(var + eps) * g + b

        def _mlla_forward(x, cpe1_w, cpe1_b, norm1_g, norm1_b, in_w, in_b, actp_w, actp_b, dwc_w, dwc_b, qk_w, qk_b, lepe_w, lepe_b, out_w, out_b, cpe2_w, cpe2_b, norm2_g, norm2_b, fc1_w, fc1_b, fc2_w, fc2_b):
            b, n, c = x.shape
            h, d = (H, c // H)
            x = x + _dwconv(x.transpose(0, 2, 1), cpe1_w, cpe1_b).transpose(0, 2, 1)
            shortcut = x
            xn = _ln(x, norm1_g, norm1_b)
            act_res = jax.nn.silu(xn @ actp_w + actp_b)
            xi = xn @ in_w + in_b
            xi = jax.nn.silu(_dwconv(xi.transpose(0, 2, 1), dwc_w, dwc_b)).transpose(0, 2, 1)
            qk = xi @ qk_w + qk_b
            q = jax.nn.elu(qk[..., :c]) + 1.0
            k = jax.nn.elu(qk[..., c:]) + 1.0
            q_rope = _rope(q).reshape(b, n, h, d).transpose(0, 2, 1, 3)
            k_rope = _rope(k).reshape(b, n, h, d).transpose(0, 2, 1, 3)
            qh = q.reshape(b, n, h, d).transpose(0, 2, 1, 3)
            kh = k.reshape(b, n, h, d).transpose(0, 2, 1, 3)
            vh = xi.reshape(b, n, h, d).transpose(0, 2, 1, 3)
            k_mean = kh.mean(axis=2, keepdims=True)
            z = 1.0 / (jnp.einsum('bhnd,bhmd->bhnm', qh, k_mean) + 1e-06)
            kv = jnp.einsum('bhnd,bhne->bhde', k_rope, vh) * (1.0 / n)
            attn = jnp.einsum('bhnd,bhde->bhne', q_rope, kv) * z
            attn = attn.transpose(0, 2, 1, 3).reshape(b, n, c)
            v_bcl = vh.transpose(0, 2, 1, 3).reshape(b, n, c).transpose(0, 2, 1)
            attn = attn + _dwconv(v_bcl, lepe_w, lepe_b).transpose(0, 2, 1)
            x = shortcut + attn * act_res @ out_w + out_b
            x = x + _dwconv(x.transpose(0, 2, 1), cpe2_w, cpe2_b).transpose(0, 2, 1)
            xn2 = _ln(x, norm2_g, norm2_b)
            mlp = jax.nn.gelu(xn2 @ fc1_w + fc1_b, approximate=False) @ fc2_w + fc2_b
            return x + mlp
        key = jax.random.key(seed)
        ks = jax.random.split(key, 12)

        def nrm(k, shape, scale=0.02):
            return jax.random.normal(k, shape, jnp.float32) * scale
        return {'x': jax.random.normal(ks[0], (B, L, C), jnp.float32), 'cpe1_w': nrm(ks[1], (C, 1, 3), 0.1), 'cpe1_b': jnp.zeros((C,), jnp.float32), 'norm1_g': jnp.ones((C,), jnp.float32), 'norm1_b': jnp.zeros((C,), jnp.float32), 'in_w': nrm(ks[2], (C, C)), 'in_b': jnp.zeros((C,), jnp.float32), 'actp_w': nrm(ks[3], (C, C)), 'actp_b': jnp.zeros((C,), jnp.float32), 'dwc_w': nrm(ks[4], (C, 1, 3), 0.1), 'dwc_b': jnp.zeros((C,), jnp.float32), 'qk_w': nrm(ks[5], (C, 2 * C)), 'qk_b': jnp.zeros((2 * C,), jnp.float32), 'lepe_w': nrm(ks[6], (C, 1, 3), 0.1), 'lepe_b': jnp.zeros((C,), jnp.float32), 'out_w': nrm(ks[7], (C, C)), 'out_b': jnp.zeros((C,), jnp.float32), 'cpe2_w': nrm(ks[8], (C, 1, 3), 0.1), 'cpe2_b': jnp.zeros((C,), jnp.float32), 'norm2_g': jnp.ones((C,), jnp.float32), 'norm2_b': jnp.zeros((C,), jnp.float32), 'fc1_w': nrm(ks[9], (C, HID)), 'fc1_b': jnp.zeros((HID,), jnp.float32), 'fc2_w': nrm(ks[10], (HID, C)), 'fc2_b': jnp.zeros((C,), jnp.float32)}
    _L1_attn_a_in = _L1_attn_a_setup()

    def _L1_attn_b_setup():
        import jax, jax.numpy as jnp
        import numpy as np
        NUM_HEADS = 16
        PAD_ID = 0.0
        key = jax.random.key(seed)
        ks = jax.random.split(key, 9)
        B, T, C = (2, 256, 128)
        x = jax.random.normal(ks[0], (B, T, C), dtype=jnp.float32)
        lim = (6.0 / (C + C)) ** 0.5

        def w(k):
            return jax.random.uniform(k, (C, C), dtype=jnp.float32, minval=-lim, maxval=lim)

        def b(k):
            return jax.random.uniform(k, (C,), dtype=jnp.float32)
        return {'x': x, 'wq_w': w(ks[1]), 'wq_b': b(ks[2]), 'wk_w': w(ks[3]), 'wk_b': b(ks[4]), 'wv_w': w(ks[5]), 'wv_b': b(ks[6]), 'wo_w': w(ks[7]), 'wo_b': b(ks[8])}
    _L1_attn_b_in = _L1_attn_b_setup()

    def _L1_ffn_setup():
        import jax, jax.numpy as jnp
        import numpy as np
        B, S, H = (2, 128, 128)
        E, F = (8, 512)
        GATE_TEMP = 0.1
        key = jax.random.key(seed)
        ks = jax.random.split(key, 6)
        s_h = 1.0 / np.sqrt(H)
        s_f = 1.0 / np.sqrt(F)
        return {'hidden_states': jax.random.normal(ks[0], (B, S, H), dtype=jnp.float32), 'w_router': jax.random.normal(ks[1], (H, E), dtype=jnp.float32) * s_h, 'w_gating': jax.random.normal(ks[2], (H, E), dtype=jnp.float32) * s_h, 'w_gate': jax.random.normal(ks[3], (E, H, F), dtype=jnp.float32) * s_h, 'w_up': jax.random.normal(ks[4], (E, H, F), dtype=jnp.float32) * s_h, 'w_down': jax.random.normal(ks[5], (E, F, H), dtype=jnp.float32) * s_f}
    _L1_ffn_in = _L1_ffn_setup()
    _d = {'L0_attn_a_X': _L0_attn_a_in['X'], 'L0_attn_a_Wq': _L0_attn_a_in['Wq'], 'L0_attn_a_Wk': _L0_attn_a_in['Wk'], 'L0_attn_a_Wv': _L0_attn_a_in['Wv'], 'L0_attn_a_Wpost': _L0_attn_a_in['Wpost'], 'L0_attn_b_Wq': _L0_attn_b_in['Wq'], 'L0_attn_b_Wk': _L0_attn_b_in['Wk'], 'L0_attn_b_Wv': _L0_attn_b_in['Wv'], 'L0_attn_b_Wo': _L0_attn_b_in['Wo'], 'L0_attn_b_lambda_q1': _L0_attn_b_in['lambda_q1'], 'L0_attn_b_lambda_k1': _L0_attn_b_in['lambda_k1'], 'L0_attn_b_lambda_q2': _L0_attn_b_in['lambda_q2'], 'L0_attn_b_lambda_k2': _L0_attn_b_in['lambda_k2'], 'L0_attn_b_gamma': _L0_attn_b_in['gamma'], 'L0_attn_b_beta': _L0_attn_b_in['beta'], 'L0_ffn_W_r': _L0_ffn_in['W_r'], 'L0_ffn_W_k': _L0_ffn_in['W_k'], 'L0_ffn_W_v': _L0_ffn_in['W_v'], 'L0_ffn_mu_r': _L0_ffn_in['mu_r'], 'L0_ffn_mu_k': _L0_ffn_in['mu_k'], 'L1_attn_a_cpe1_w': _L1_attn_a_in['cpe1_w'], 'L1_attn_a_cpe1_b': _L1_attn_a_in['cpe1_b'], 'L1_attn_a_norm1_g': _L1_attn_a_in['norm1_g'], 'L1_attn_a_norm1_b': _L1_attn_a_in['norm1_b'], 'L1_attn_a_in_w': _L1_attn_a_in['in_w'], 'L1_attn_a_in_b': _L1_attn_a_in['in_b'], 'L1_attn_a_actp_w': _L1_attn_a_in['actp_w'], 'L1_attn_a_actp_b': _L1_attn_a_in['actp_b'], 'L1_attn_a_dwc_w': _L1_attn_a_in['dwc_w'], 'L1_attn_a_dwc_b': _L1_attn_a_in['dwc_b'], 'L1_attn_a_qk_w': _L1_attn_a_in['qk_w'], 'L1_attn_a_qk_b': _L1_attn_a_in['qk_b'], 'L1_attn_a_lepe_w': _L1_attn_a_in['lepe_w'], 'L1_attn_a_lepe_b': _L1_attn_a_in['lepe_b'], 'L1_attn_a_out_w': _L1_attn_a_in['out_w'], 'L1_attn_a_out_b': _L1_attn_a_in['out_b'], 'L1_attn_a_cpe2_w': _L1_attn_a_in['cpe2_w'], 'L1_attn_a_cpe2_b': _L1_attn_a_in['cpe2_b'], 'L1_attn_a_norm2_g': _L1_attn_a_in['norm2_g'], 'L1_attn_a_norm2_b': _L1_attn_a_in['norm2_b'], 'L1_attn_a_fc1_w': _L1_attn_a_in['fc1_w'], 'L1_attn_a_fc1_b': _L1_attn_a_in['fc1_b'], 'L1_attn_a_fc2_w': _L1_attn_a_in['fc2_w'], 'L1_attn_a_fc2_b': _L1_attn_a_in['fc2_b'], 'L1_attn_b_wq_w': _L1_attn_b_in['wq_w'], 'L1_attn_b_wq_b': _L1_attn_b_in['wq_b'], 'L1_attn_b_wk_w': _L1_attn_b_in['wk_w'], 'L1_attn_b_wk_b': _L1_attn_b_in['wk_b'], 'L1_attn_b_wv_w': _L1_attn_b_in['wv_w'], 'L1_attn_b_wv_b': _L1_attn_b_in['wv_b'], 'L1_attn_b_wo_w': _L1_attn_b_in['wo_w'], 'L1_attn_b_wo_b': _L1_attn_b_in['wo_b'], 'L1_ffn_w_router': _L1_ffn_in['w_router'], 'L1_ffn_w_gating': _L1_ffn_in['w_gating'], 'L1_ffn_w_gate': _L1_ffn_in['w_gate'], 'L1_ffn_w_up': _L1_ffn_in['w_up'], 'L1_ffn_w_down': _L1_ffn_in['w_down']}
    _x0 = _d['L0_attn_a_X']
    _d['L0_attn_a_X'] = jax.random.normal(jax.random.fold_in(jax.random.key(seed), 1), (4, 512, 128), dtype=_x0.dtype)
    del _x0
    return _d

def reference(L0_attn_a_X, L0_attn_a_Wq, L0_attn_a_Wk, L0_attn_a_Wv, L0_attn_a_Wpost, L0_attn_b_Wq, L0_attn_b_Wk, L0_attn_b_Wv, L0_attn_b_Wo, L0_attn_b_lambda_q1, L0_attn_b_lambda_k1, L0_attn_b_lambda_q2, L0_attn_b_lambda_k2, L0_attn_b_gamma, L0_attn_b_beta, L0_ffn_W_r, L0_ffn_W_k, L0_ffn_W_v, L0_ffn_mu_r, L0_ffn_mu_k, L1_attn_a_cpe1_w, L1_attn_a_cpe1_b, L1_attn_a_norm1_g, L1_attn_a_norm1_b, L1_attn_a_in_w, L1_attn_a_in_b, L1_attn_a_actp_w, L1_attn_a_actp_b, L1_attn_a_dwc_w, L1_attn_a_dwc_b, L1_attn_a_qk_w, L1_attn_a_qk_b, L1_attn_a_lepe_w, L1_attn_a_lepe_b, L1_attn_a_out_w, L1_attn_a_out_b, L1_attn_a_cpe2_w, L1_attn_a_cpe2_b, L1_attn_a_norm2_g, L1_attn_a_norm2_b, L1_attn_a_fc1_w, L1_attn_a_fc1_b, L1_attn_a_fc2_w, L1_attn_a_fc2_b, L1_attn_b_wq_w, L1_attn_b_wq_b, L1_attn_b_wk_w, L1_attn_b_wk_b, L1_attn_b_wv_w, L1_attn_b_wv_b, L1_attn_b_wo_w, L1_attn_b_wo_b, L1_ffn_w_router, L1_ffn_w_gating, L1_ffn_w_gate, L1_ffn_w_up, L1_ffn_w_down):

    def _L0_attn_a_ref(X, Wq, Wk, Wv, Wpost):
        import jax, jax.numpy as jnp
        import numpy as np
        import math
        INPUT_WIDTH = 128
        KEY_WIDTH = 64
        VALUE_WIDTH = 64
        NUM_HEADS = 16
        NUM_GROUPS = 4
        HEADS_PER_GROUP = NUM_HEADS // NUM_GROUPS
        n, s, _ = X.shape
        Q = (X @ Wq).reshape(n, s, NUM_GROUPS, HEADS_PER_GROUP, KEY_WIDTH)
        K = (X @ Wk).reshape(n, s, NUM_GROUPS, KEY_WIDTH)
        V = (X @ Wv).reshape(n, s, NUM_GROUPS, VALUE_WIDTH)
        scale = 1.0 / math.sqrt(KEY_WIDTH)
        raw = jnp.einsum('bsgwe,btge->bstgw', Q, K * scale)
        attn = jax.nn.softmax(raw, axis=2)
        A = jnp.einsum('bstgw,btge->bsgwe', attn, V).reshape(n, s, NUM_HEADS * VALUE_WIDTH)
        P = A @ Wpost
        return X + P

    def _L0_attn_b_ref(x, Wq, Wk, Wv, Wo, lambda_q1, lambda_k1, lambda_q2, lambda_k2, gamma, beta):
        import jax, jax.numpy as jnp
        import numpy as np
        import math
        DIM = 128
        NUM_HEADS = 16
        HEAD_DIM = DIM // NUM_HEADS
        LAYER_IDX = 12
        LAMBDA_INIT = 0.8 - 0.6 * math.exp(-0.3 * (LAYER_IDX - 1))
        LN_EPS = 1e-05
        B, S, _ = x.shape
        scaling = HEAD_DIM ** (-0.5)
        Q = (x @ Wq).reshape(B, S, NUM_HEADS, 2 * HEAD_DIM).transpose(0, 2, 1, 3)
        K = (x @ Wk).reshape(B, S, NUM_HEADS, 2 * HEAD_DIM).transpose(0, 2, 1, 3)
        V = (x @ Wv).reshape(B, S, NUM_HEADS, HEAD_DIM).transpose(0, 2, 1, 3)
        lamb = jnp.exp(jnp.sum(lambda_q1 * lambda_k1)) - jnp.exp(jnp.sum(lambda_q2 * lambda_k2)) + LAMBDA_INIT
        Q1, Q2 = jnp.split(Q, 2, axis=-1)
        K1, K2 = jnp.split(K, 2, axis=-1)
        A1 = jnp.einsum('bhqd,bhkd->bhqk', Q1, K1) * scaling
        A2 = jnp.einsum('bhqd,bhkd->bhqk', Q2, K2) * scaling
        attn = jax.nn.softmax(A1, axis=-1) - lamb * jax.nn.softmax(A2, axis=-1)
        out = jnp.einsum('bhqk,bhkd->bhqd', attn, V)
        out = out.transpose(0, 2, 1, 3).reshape(B, S, DIM)
        out = out @ Wo
        mu = jnp.mean(out, axis=-1, keepdims=True)
        var = jnp.var(out, axis=-1, keepdims=True)
        out = (out - mu) * jax.lax.rsqrt(var + LN_EPS) * gamma + beta
        return out

    def _L0_ffn_ref(x, W_r, W_k, W_v, mu_r, mu_k):
        import jax, jax.numpy as jnp
        import numpy as np
        DIM = 128

        def _reference_tuple_inner(x, W_r, W_k, W_v, mu_r, mu_k):
            B, T, C = x.shape
            x_prev = jnp.concatenate([jnp.zeros((B, 1, C), x.dtype), x[:, :-1, :]], axis=1)
            xr = mu_r * x + (1.0 - mu_r) * x_prev
            xk = mu_k * x + (1.0 - mu_k) * x_prev
            r = jax.nn.sigmoid(jnp.einsum('btc,dc->btd', xr, W_r))
            k = jnp.einsum('btc,dc->btd', xk, W_k)
            k_act = jnp.square(jax.nn.relu(k))
            out = r * jnp.einsum('btc,dc->btd', k_act, W_v)
            new_state = x[:, -1, :]
            return (out, new_state)
        return _reference_tuple_inner(x, W_r, W_k, W_v, mu_r, mu_k)[0]

    def _L1_attn_a_ref(x, cpe1_w, cpe1_b, norm1_g, norm1_b, in_w, in_b, actp_w, actp_b, dwc_w, dwc_b, qk_w, qk_b, lepe_w, lepe_b, out_w, out_b, cpe2_w, cpe2_b, norm2_g, norm2_b, fc1_w, fc1_b, fc2_w, fc2_b):
        import jax, jax.numpy as jnp
        import numpy as np
        B, L, C, H = (8, 256, 128, 16)
        HID = 4 * C

        def _rope(x):
            b, n, c = x.shape
            k_max = c // 2
            theta = 1.0 / 10000.0 ** (jnp.arange(k_max, dtype=jnp.float32) / k_max)
            cos_t, sin_t = (jnp.cos(theta), jnp.sin(theta))
            xr = x.reshape(b, n, k_max, 2)
            re = xr[..., 0] * cos_t - xr[..., 1] * sin_t
            im = xr[..., 0] * sin_t + xr[..., 1] * cos_t
            return jnp.stack((re, im), axis=-1).reshape(b, n, c)

        def _dwconv(x_bcl, w, bias):
            y = jax.lax.conv_general_dilated(x_bcl, w, (1,), [(1, 1)], dimension_numbers=('NCH', 'OIH', 'NCH'), feature_group_count=x_bcl.shape[1])
            return y + bias[None, :, None]

        def _ln(x, g, b, eps=1e-05):
            mu = x.mean(-1, keepdims=True)
            var = ((x - mu) ** 2).mean(-1, keepdims=True)
            return (x - mu) * jax.lax.rsqrt(var + eps) * g + b

        def _mlla_forward(x, cpe1_w, cpe1_b, norm1_g, norm1_b, in_w, in_b, actp_w, actp_b, dwc_w, dwc_b, qk_w, qk_b, lepe_w, lepe_b, out_w, out_b, cpe2_w, cpe2_b, norm2_g, norm2_b, fc1_w, fc1_b, fc2_w, fc2_b):
            b, n, c = x.shape
            h, d = (H, c // H)
            x = x + _dwconv(x.transpose(0, 2, 1), cpe1_w, cpe1_b).transpose(0, 2, 1)
            shortcut = x
            xn = _ln(x, norm1_g, norm1_b)
            act_res = jax.nn.silu(xn @ actp_w + actp_b)
            xi = xn @ in_w + in_b
            xi = jax.nn.silu(_dwconv(xi.transpose(0, 2, 1), dwc_w, dwc_b)).transpose(0, 2, 1)
            qk = xi @ qk_w + qk_b
            q = jax.nn.elu(qk[..., :c]) + 1.0
            k = jax.nn.elu(qk[..., c:]) + 1.0
            q_rope = _rope(q).reshape(b, n, h, d).transpose(0, 2, 1, 3)
            k_rope = _rope(k).reshape(b, n, h, d).transpose(0, 2, 1, 3)
            qh = q.reshape(b, n, h, d).transpose(0, 2, 1, 3)
            kh = k.reshape(b, n, h, d).transpose(0, 2, 1, 3)
            vh = xi.reshape(b, n, h, d).transpose(0, 2, 1, 3)
            k_mean = kh.mean(axis=2, keepdims=True)
            z = 1.0 / (jnp.einsum('bhnd,bhmd->bhnm', qh, k_mean) + 1e-06)
            kv = jnp.einsum('bhnd,bhne->bhde', k_rope, vh) * (1.0 / n)
            attn = jnp.einsum('bhnd,bhde->bhne', q_rope, kv) * z
            attn = attn.transpose(0, 2, 1, 3).reshape(b, n, c)
            v_bcl = vh.transpose(0, 2, 1, 3).reshape(b, n, c).transpose(0, 2, 1)
            attn = attn + _dwconv(v_bcl, lepe_w, lepe_b).transpose(0, 2, 1)
            x = shortcut + attn * act_res @ out_w + out_b
            x = x + _dwconv(x.transpose(0, 2, 1), cpe2_w, cpe2_b).transpose(0, 2, 1)
            xn2 = _ln(x, norm2_g, norm2_b)
            mlp = jax.nn.gelu(xn2 @ fc1_w + fc1_b, approximate=False) @ fc2_w + fc2_b
            return x + mlp
        return _mlla_forward(x, cpe1_w, cpe1_b, norm1_g, norm1_b, in_w, in_b, actp_w, actp_b, dwc_w, dwc_b, qk_w, qk_b, lepe_w, lepe_b, out_w, out_b, cpe2_w, cpe2_b, norm2_g, norm2_b, fc1_w, fc1_b, fc2_w, fc2_b)

    def _L1_attn_b_ref(x, wq_w, wq_b, wk_w, wk_b, wv_w, wv_b, wo_w, wo_b):
        import jax, jax.numpy as jnp
        import numpy as np
        NUM_HEADS = 16
        PAD_ID = 0.0
        B, T, C = x.shape
        H = NUM_HEADS
        Dh = C // H
        scale = Dh ** (-0.5)
        q = (x @ wq_w.T + wq_b).reshape(B, T, H, Dh)
        k = (x @ wk_w.T + wk_b).reshape(B, T, H, Dh)
        v = (x @ wv_w.T + wv_b).reshape(B, T, H, Dh)
        scores = jnp.einsum('bthd,bshd->bhts', q, k) * scale
        key_mask = (x[:, :, 0] != PAD_ID)[:, None, None, :]
        scores = jnp.where(key_mask, scores, -jnp.inf)
        attn = jax.nn.softmax(scores, axis=-1)
        out = jnp.einsum('bhts,bshd->bthd', attn, v).reshape(B, T, C)
        return out @ wo_w.T + wo_b

    def _L1_ffn_ref(hidden_states, w_router, w_gating, w_gate, w_up, w_down):
        import jax, jax.numpy as jnp
        import numpy as np
        B, S, H = (2, 128, 128)
        E, F = (8, 512)
        GATE_TEMP = 0.1
        x = hidden_states
        router_probs = jax.nn.softmax(jnp.einsum('bsh,he->bse', x, w_router), axis=-1)
        gate_weights = jax.nn.softmax(jnp.einsum('bsh,he->bse', x, w_gating) / GATE_TEMP, axis=-1)
        g = jnp.einsum('bsh,ehf->ebsf', x, w_gate)
        u = jnp.einsum('bsh,ehf->ebsf', x, w_up)
        h = jax.nn.silu(g) * u
        expert_out = jnp.einsum('ebsf,efh->ebsh', h, w_down)
        cw = router_probs * gate_weights
        cw = cw / (jnp.sum(cw, axis=-1, keepdims=True) + 1e-09)
        out = jnp.einsum('ebsh,bse->bsh', expert_out, cw)
        return out
    x = L0_attn_a_X
    x = x + _L0_attn_a_ref(_layernorm(x, axis=-1), L0_attn_a_Wq, L0_attn_a_Wk, L0_attn_a_Wv, L0_attn_a_Wpost)
    x = x + _L0_ffn_ref(_layernorm(x, axis=-1), L0_ffn_W_r, L0_ffn_W_k, L0_ffn_W_v, L0_ffn_mu_r, L0_ffn_mu_k)
    x = x + _L0_attn_b_ref(_layernorm(x, axis=-1), L0_attn_b_Wq, L0_attn_b_Wk, L0_attn_b_Wv, L0_attn_b_Wo, L0_attn_b_lambda_q1, L0_attn_b_lambda_k1, L0_attn_b_lambda_q2, L0_attn_b_lambda_k2, L0_attn_b_gamma, L0_attn_b_beta)
    x = x + _L0_ffn_ref(_layernorm(x, axis=-1), L0_ffn_W_r, L0_ffn_W_k, L0_ffn_W_v, L0_ffn_mu_r, L0_ffn_mu_k)
    x = x + _L1_attn_a_ref(_layernorm(x, axis=-1), L1_attn_a_cpe1_w, L1_attn_a_cpe1_b, L1_attn_a_norm1_g, L1_attn_a_norm1_b, L1_attn_a_in_w, L1_attn_a_in_b, L1_attn_a_actp_w, L1_attn_a_actp_b, L1_attn_a_dwc_w, L1_attn_a_dwc_b, L1_attn_a_qk_w, L1_attn_a_qk_b, L1_attn_a_lepe_w, L1_attn_a_lepe_b, L1_attn_a_out_w, L1_attn_a_out_b, L1_attn_a_cpe2_w, L1_attn_a_cpe2_b, L1_attn_a_norm2_g, L1_attn_a_norm2_b, L1_attn_a_fc1_w, L1_attn_a_fc1_b, L1_attn_a_fc2_w, L1_attn_a_fc2_b)
    x = x + _L1_ffn_ref(_layernorm(x, axis=-1), L1_ffn_w_router, L1_ffn_w_gating, L1_ffn_w_gate, L1_ffn_w_up, L1_ffn_w_down)
    x = x + _L1_attn_b_ref(_layernorm(x, axis=-1), L1_attn_b_wq_w, L1_attn_b_wq_b, L1_attn_b_wk_w, L1_attn_b_wk_b, L1_attn_b_wv_w, L1_attn_b_wv_b, L1_attn_b_wo_w, L1_attn_b_wo_b)
    x = x + _L1_ffn_ref(_layernorm(x, axis=-1), L1_ffn_w_router, L1_ffn_w_gating, L1_ffn_w_gate, L1_ffn_w_up, L1_ffn_w_down)
    return x

_drawn_inputs = setup_inputs


def setup_inputs(seed=0):
    import zlib

    import numpy as np

    out = dict(_drawn_inputs(seed))
    spreads = {'L0_attn_b_gamma': (1.0, 0.2),
     'L0_attn_b_beta': (0.0, 0.449),
     'L1_attn_a_cpe1_b': (0.0, 0.1),
     'L1_attn_a_norm1_g': (1.0, 0.6),
     'L1_attn_a_norm1_b': (0.0, 0.8),
     'L1_attn_a_in_b': (0.0, 0.8),
     'L1_attn_a_actp_b': (0.0, 0.8),
     'L1_attn_a_dwc_b': (0.0, 0.8),
     'L1_attn_a_qk_b': (0.0, 2.0),
     'L1_attn_a_lepe_b': (0.0, 0.8),
     'L1_attn_a_out_b': (0.0, 0.8),
     'L1_attn_a_cpe2_b': (0.0, 0.8),
     'L1_attn_a_norm2_g': (1.0, 0.6),
     'L1_attn_a_norm2_b': (0.0, 2.0),
     'L1_attn_a_fc1_b': (0.0, 2.0),
     'L1_attn_a_fc2_b': (0.0, 0.8)}
    factors = {'L0_attn_a_Wq': 6.845,
     'L0_attn_a_Wk': 7.024,
     'L0_attn_a_Wv': 4.3,
     'L0_attn_a_Wpost': 4.485,
     'L0_attn_b_lambda_q1': 8.0,
     'L0_attn_b_lambda_k1': 5.528,
     'L0_attn_b_lambda_q2': 25.448,
     'L0_attn_b_lambda_k2': 22.968,
     'L0_ffn_W_r': 2.934,
     'L0_ffn_mu_r': 17.8,
     'L1_attn_a_in_w': 8.0,
     'L1_attn_a_actp_w': 8.0,
     'L1_attn_a_dwc_w': 8.0,
     'L1_attn_a_qk_w': 8.0,
     'L1_attn_a_lepe_w': 8.0,
     'L1_attn_a_out_w': 8.0,
     'L1_attn_a_fc1_w': 9.836,
     'L1_attn_b_wq_b': 21.013,
     'L1_attn_b_wk_b': 64.0,
     'L1_attn_b_wq_w': 5.963,
     'L1_attn_b_wv_b': 3.548,
     'L1_attn_b_wo_b': 3.529,
     'L1_ffn_w_router': 4.748}
    for name, (base, spread) in spreads.items():
        noise = np.random.default_rng([zlib.crc32(name.encode()), seed]).standard_normal(out[name].shape)
        drawn = base * np.exp(spread * noise) if base else spread * noise
        out[name] = jnp.asarray(drawn.astype(out[name].dtype))
    for name, factor in factors.items():
        out[name] = (out[name] * factor).astype(out[name].dtype)
    return out
```

```python
from contextlib import ExitStack

import numpy as np

import concourse.bass as bass
from concourse import mybir

P = 128
C = 128
B = 4
T = 512
N = B * T
NT = N // P
TPC = T // P
HH = 4
D8 = 8
DA = 64
NE = 8
FF = 512
FB = FF // P
UNITS = HH * TPC
LEAD_A = 3
LEAD_N = 6
SPLIT8 = 3
ROWS8 = SPLIT8 * SPLIT8 * D8
SHIFT8 = 96
NSH = 2 * HH
EPS = 1e-5

F32 = mybir.dt.float32
BF16 = mybir.dt.bfloat16
ALU = mybir.AluOpType
ACT = mybir.ActivationFunctionType
AX = mybir.AxisListType

W_COLS = [
    ("a_wq", 1024), ("a_wk", 256), ("a_wv", 256), ("a_wpost", 1024),
    ("b_wq", 256), ("b_wk", 256), ("b_wv", 128), ("b_wo", 1024),
    ("c_wq", 128), ("c_wk", 128), ("c_wv", 128), ("c_wo", 512), ("c_vb", 128),
    ("f_wr", 128), ("f_wk", 128), ("f_wv", 128),
    ("m_in", 128), ("m_actp", 128), ("m_qk", 256), ("m_out", 128), ("m_fc1", 512), ("m_fc2", 512),
    ("e_route", 16), ("lam", 4 * D8),
]
K_COLS = [("ident", 128), ("mean", 128), ("rope", 128), ("ropeT", 128), ("block", 128), ("pick", 6)]
V_COLS = [
    "f_mur", "f_muk", "c_qb", "c_kb", "c_ob", "b_gamma", "b_beta",
    "cpe1_w0", "cpe1_w1", "cpe1_w2", "cpe1_b", "n1_g", "n1_b", "in_b", "actp_b",
    "dwc_w0", "dwc_w1", "dwc_w2", "dwc_b", "q_b", "k_b", "lepe_w0", "lepe_w1", "lepe_w2", "lepe_b",
    "out_b", "cpe2_w0", "cpe2_w1", "cpe2_w2", "cpe2_b", "n2_g", "n2_b",
    "fc1_b0", "fc1_b1", "fc1_b2", "fc1_b3", "fc2_b", "odd", "zero", "eps", "tiny",
]
LAMBDA_INIT = 0.8 - 0.6 * float(np.exp(-0.3 * 11))


def offsets(cols):
    at, out = 0, {}
    for name, n in cols:
        out[name] = (at, n)
        at += n
    return out, at


def run_groups(eng, ng, body, head=2, tail=2):
    loops = (ng - head - tail) // 3
    for g in range(head):
        body(g, g % 3, g // 3)
    with eng.Fori(0, loops) as t:
        for q in range(head, head + 3):
            body(3 * t + q, q % 3, t + q // 3)
    for g in range(3 * loops + head, ng):
        body(g, g % 3, g // 3)


def build(nc, x_in, wts, cst, vec, moe_w, stack_const, ident_bf, out):
    wofs, wn = offsets(W_COLS)
    kofs, kn = offsets(K_COLS)
    with ExitStack() as ctx:
        def sb(name, shape, dt=F32):
            return ctx.enter_context(nc.sbuf_tensor(name, shape, dt))

        sems = {}

        def sem(name):
            if name not in sems:
                sems[name] = ctx.enter_context(nc.semaphore(name))
            return sems[name]

        def dram(name, shape, dt):
            return nc.dram_tensor(name, shape, dt, kind="Internal").ap()

        a_q = dram("a_q", (16, 2, DA, HH, T), BF16)
        a_k = dram("a_k", (16, 2, DA, T), BF16)
        a_v = dram("a_v", (16, P, TPC, DA), F32)
        n_q = dram("n_q", (32, SPLIT8, D8, HH, T), BF16)
        n_k = dram("n_k", (32, SPLIT8, D8, HH, T), BF16)
        n_mask = dram("n_mask", (B, T), BF16)

        x = sb("x", [P, N])
        xn = sb("xn", [P, N])
        u_buf = sb("u_buf", [P, 2 * N])
        sq = sb("sq", [P, N])
        std = sb("std", [P, N])
        pbuf = sb("pbuf", [P, 8, T])
        parts_out = sb("parts_out", [P, 4, SPLIT8, T], BF16)
        arena = sb("arena", [P, 6 * N])
        wsb = sb("wsb", [P, wn])
        ksb = sb("ksb", [P, kn])
        vsb = sb("vsb", [P, len(V_COLS)])
        moe = sb("moe", [P, 3, NE, FF])
        identb = sb("identb", [P, P], BF16)
        wog = xn[:, 0:6 * P].rearrange("p (m n) -> p m n", m=3)
        osum = sq[:, 0:2 * T].rearrange("p (s t) -> p s t", s=2)
        onorm = std[:, 0:2 * T].rearrange("p (s t) -> p s t", s=2)
        maskrow = sq[:, N // 2:N].bitcast(BF16)
        mx = sb("mx", [P, UNITS])
        shift = sb("shift", [P, TPC, 2, HH], BF16)
        small = sb("small", [P, 64])
        dev = sb("dev", [P, NT])
        rdev = sb("rdev", [P, NT])
        rsum = sb("rsum", [P, UNITS])
        ps = ctx.enter_context(nc.psum_tensor("ps", [P, 8, T], F32))

        def w(name, a=0, n=None):
            o, full = wofs[name]
            return wsb[:, o + a:o + a + (full - a if n is None else n)]

        def k(name):
            o, n = kofs[name]
            return ksb[:, o:o + n]

        def v(name):
            i = V_COLS.index(name)
            return vsb[:, i:i + 1]

        def ch(t, c):
            return t[:, c * T:(c + 1) * T]

        def bf_view(at, n):
            return arena[:, at:at + n // 2].bitcast(BF16)

        st_a = [bf_view(1024 * i, 2048).rearrange("p (h t) -> p h t", h=HH) for i in range(3)]
        st_b = [bf_view(3072 + 1024 * i, 2048).rearrange("p (h t) -> p h t", h=HH) for i in range(3)]
        st_c = [bf_view(6144 + 1024 * i, 2048).rearrange("p (h t) -> p h t", h=HH) for i in range(3)]
        ka = [bf_view(9216 + 256 * i, 512) for i in range(3)]
        va = [arena[:, 9984 + 768 * i:9984 + 768 * (i + 1)].rearrange("p (k n) -> p k n", k=TPC) for i in range(3)]
        vn = [arena[:, 9984 + 512 * i:9984 + 512 * (i + 1)].rearrange("p (k h n) -> p k h n", k=TPC, h=HH)
              for i in range(3)]
        tmp = [arena[:, i * N:(i + 1) * N] for i in range(6)]
        ub = [u_buf[:, 0:N], u_buf[:, N:2 * N]]
        pflat = pbuf[:, :, :].rearrange("p s t -> p (s t)")
        pb = [pflat[:, 0:N], pflat[:, N:2 * N]]
        v_wide = u_buf[:, :].rearrange("p (t n) -> p t n", t=NT)
        v_narrow = ub[0].rearrange("p (t n) -> p t n", t=NT)
        acc_narrow = ub[1]

        bankA = [ps[:, c, :] for c in range(4)]
        bankB = [ps[:, 4 + c, :] for c in range(4)]
        score = [ps[:, i, :] for i in range(2)]
        tscore = [ps[:, 2 + i, :] for i in range(2)]
        o_bank = [ps[:, 4 + i, :] for i in range(2)]
        sh_bank, pr_bank = ps[:, 6, :], ps[:, 7, :]
        n_score = [ps[:, i, :] for i in range(3)]
        n_tscore = [ps[:, 3 + i, :] for i in range(3)]
        n_o, n_x = ps[:, 6, :], ps[:, 7, :]

        block = ctx.enter_context(nc.Block())
        dchain = [0]

        def link(dve, ins):
            dchain[0] += 1
            ins.then_inc(sem("dve_chain"), 1)
            dve.wait_ge(sem("dve_chain"), dchain[0])

        def stage_end(eng, s):
            eng.drain().then_inc(sem("stage_done"), 1)
            eng.wait_ge(sem("stage_done"), 5 * s)

        def ln_pe(pe, i, src, src_ready=None):
            for c in range(B):
                if src_ready:
                    pe.wait_ge(sem(src_ready), c + 1)
                nc.tensor.matmul(bankA[c], k("mean"), ch(src, c), start=True, stop=True).then_inc(sem("ln_mean"), 1)
            for c in range(B):
                pe.wait_ge(sem("ln_sq"), B * i + c + 1)
                for j in range(TPC):
                    last = nc.tensor.matmul(bankB[c][:, j:j + 1], sq[:, c * T + j * P:c * T + (j + 1) * P],
                                            k("mean")[:, 0:1], start=True, stop=True)
                last.then_inc(sem("ln_var"), 1)
            for c in range(B):
                pe.wait_ge(sem("ln_rec"), B * i + c + 1)
                for j in range(TPC):
                    t = TPC * c + j
                    last = nc.tensor.matmul(bankB[c][:, j * P:(j + 1) * P], rdev[:, t:t + 1].broadcast_to([P, P]),
                                            k("ident"), start=True, stop=True)
                last.then_inc(sem("ln_bc"), 1)

        def ln_act(act, i, dst):
            for c in range(B):
                act.wait_ge(sem("ln_cent"), B * i + c + 1)
                nc.scalar.activation(ch(sq, c), ch(dst, c), ACT.Square).then_inc(sem("ln_sq"), 1)
            for c in range(B):
                act.wait_ge(sem("ln_var"), B * i + c + 1)
                nc.scalar.activation(dev[:, TPC * c:TPC * (c + 1)], bankB[c][:, 0:TPC], ACT.Sqrt, bias=v("eps")) \
                    .then_inc(sem("ln_std"), 1)

        def ln_dve(dve, i, src, dst, g=None, b=None):
            for c in range(B):
                dve.wait_ge(sem("ln_mean"), B * i + c + 1)
                nc.vector.tensor_tensor(ch(dst, c), ch(src, c), bankA[c], ALU.subtract).then_inc(sem("ln_cent"), 1)
            for c in range(B):
                dve.wait_ge(sem("ln_std"), B * i + c + 1)
                nc.vector.reciprocal(rdev[:, TPC * c:TPC * (c + 1)], dev[:, TPC * c:TPC * (c + 1)]) \
                    .then_inc(sem("ln_rec"), 1)
            for c in range(B):
                dve.wait_ge(sem("ln_bc"), B * i + c + 1)
                last = nc.vector.tensor_tensor(ch(dst, c), ch(dst, c), bankB[c], ALU.mult)
                if g:
                    link(dve, last)
                    last = nc.vector.tensor_scalar(ch(dst, c), ch(dst, c), v(g), v(b), ALU.mult, ALU.add)
                last.then_inc(sem("ln_out"), 1)

        def conv_dve(dve, dst, src, c, center, left, right, bias):
            d, s = ch(dst, c), ch(src, c)
            link(dve, nc.vector.tensor_scalar(d, s, v(center), v(bias), ALU.mult, ALU.add))
            link(dve, nc.vector.scalar_tensor_tensor(d[:, 1:T], s[:, 0:T - 1], v(left), d[:, 1:T], ALU.mult, ALU.add))
            return nc.vector.scalar_tensor_tensor(d[:, 0:T - 1], s[:, 1:T], v(right), d[:, 0:T - 1],
                                                  ALU.mult, ALU.add)

        x_tok = sq[:, :].rearrange("p (t c) -> p t c", t=NT)

        def load_sp(sp):
            sp.dma_start(x_tok, x_in.rearrange("b (t p) c -> p (b t) c", p=P)).then_inc(sem("x_loaded"), 16)
            sp.dma_start(ksb[:, :], cst).then_inc(sem("const_loaded"), 16)
            sp.dma_start(vsb[:, :], vec).then_inc(sem("const_loaded"), 16)
            sp.dma_start(identb[:, :], ident_bf).then_inc(sem("const_loaded"), 16)
            sp.dma_start(wsb[:, :], wts).then_inc(sem("weights_loaded"), 16)
            sp.dma_start(moe[:, :, :, :], moe_w).then_inc(sem("moe_loaded"), 16)
            sp.wait_ge(sem("x_loaded"), 16)
            sp.wait_ge(sem("const_loaded"), 48)

        def load_pe(pe):
            pe.wait_ge(sem("x_loaded"), 16)
            pe.wait_ge(sem("const_loaded"), 48)
            for t in range(NT):
                nc.tensor.transpose(ps[:, t // TPC, (t % TPC) * P:(t % TPC + 1) * P], x_tok[:, t, :],
                                    k("ident")).then_inc(sem("x_turned"), 1)

        def load_act(act):
            for c in range(B):
                act.wait_ge(sem("x_turned"), TPC * (c + 1))
                nc.scalar.activation(ch(x, c), bankA[c], ACT.Copy).then_inc(sem("x_set"), 1)

        NQA, NKA = 8, 2
        NPA = NQA + NKA

        def aproj_pe(pe):
            ln_pe(pe, 0, x)
            pe.wait_ge(sem("weights_loaded"), 16)
            for b in range(B):
                pe.wait_ge(sem("ln_out"), b + 1)
                for j in range(NPA):
                    n = NPA * b + j
                    if n == 4:
                        pe.wait_ge(sem("ln_out"), B)
                    if n >= 8:
                        pe.wait_ge(sem("a_lo"), n - 7)
                    lhs = w("a_wq", j * P, P) if j < NQA else w("a_wk", (j - NQA) * P, P)
                    nc.tensor.matmul(ps[:, n % 8, :], lhs, ch(xn, b), start=True, stop=True).then_inc(sem("a_proj"), 1)
            for t in range(NT):
                n = NPA * B + t
                if t < 8:
                    pe.wait_ge(sem("a_lo"), n - 7)
                else:
                    pe.wait_ge(sem("a_vset"), t - 7)
                nc.tensor.matmul(ps[:, n % 8, 0:HH * DA], xn[:, t * P:(t + 1) * P], w("a_wv"), start=True,
                                 stop=True).then_inc(sem("a_vproj"), 1)

        def aproj_act(act):
            ln_act(act, 0, xn)
            for n in range(NPA * B):
                act.wait_ge(sem("a_proj"), n + 1)
                if n >= 4:
                    act.wait_ge(sem(f"a_put{n % 4}"), 16 * (n // 4))
                    act.wait_ge(sem("a_lo"), n - 3)
                nc.scalar.activation(parts_out[:, n % 4, 0, :], ps[:, n % 8, :], ACT.Copy).then_inc(sem("a_hi"), 1)
            for t in range(NT):
                act.wait_ge(sem("a_vproj"), t + 1)
                nc.scalar.activation(v_wide[:, t, :], ps[:, (NPA * B + t) % 8, 0:HH * DA],
                                     ACT.Copy).then_inc(sem("a_vset"), 1)

        def aproj_dve(dve):
            ln_dve(dve, 0, x, xn)
            for n in range(NPA * B):
                dve.wait_ge(sem("a_hi"), n + 1)
                if n >= 4:
                    dve.wait_ge(sem(f"pool_put{n % 4}"), 16 * (n // 4))
                nc.vector.tensor_tensor(parts_out[:, n % 4, 1, :], ps[:, n % 8, :], parts_out[:, n % 4, 0, :],
                                        ALU.subtract).then_inc(sem("a_lo"), 1)

        def a_store(eng, part, ready, put):
            for n in range(NPA * B):
                b, j = n // NPA, n % NPA
                eng.wait_ge(sem(ready), n + 1)
                if j < NQA:
                    dst = a_q[HH * b + j // 2, part, :, 2 * (j % 2):2 * (j % 2) + 2, :].rearrange("d h t -> h d t")
                else:
                    g = HH * b + 2 * (j - NQA)
                    dst = a_k[g:g + 2, part, :, :]
                eng.dma_start(dst, parts_out[:, n % 4, part, :]).then_inc(sem(f"{put}{n % 4}"), 16)

        def aproj_sp(sp):
            a_store(sp, 0, "a_hi", "a_put")
            for t in range(NT):
                sp.wait_ge(sem("a_vset"), t + 1)
                b, i = t // TPC, t % TPC
                sp.dma_start(a_v[HH * b:HH * b + HH, :, i, :].rearrange("g p d -> p g d"),
                             v_wide[:, t, :].rearrange("p (g d) -> p g d", g=HH)).then_inc(sem("a_vput"), 16)
            for i in range(4):
                sp.wait_ge(sem(f"a_put{i}"), 16 * NPA * B // 4)
            sp.wait_ge(sem("a_vput"), 16 * NT)

        def aproj_pool(pool):
            for c in range(B):
                pool.wait_ge(sem("ln_out"), c + 1)
                nc.gpsimd.tensor_tensor(ch(x, c), ch(x, c), ch(xn, c), ALU.add).then_inc(sem("x_plus_n"), 1)
            a_store(pool, 1, "a_lo", "pool_put")
            for i in range(4):
                pool.wait_ge(sem(f"pool_put{i}"), 16 * NPA * B // 4)

        NGA = 16

        def aload(sp, g, m):
            s = sem(f"a_got{m}")
            sp.dma_start(st_a[m], a_q[bass.ds(g, 1), 0].rearrange("g d h t -> g d (h t)").broadcast_to([2, DA, HH * T])).then_inc(s, 16)
            sp.dma_start(st_b[m][0:DA], a_q[bass.ds(g, 1), 1].rearrange("g d h t -> (g d) h t")).then_inc(s, 16)
            sp.dma_start(ka[m], a_k[bass.ds(g, 1)].rearrange("g a d t -> (g a d) t")).then_inc(s, 16)
            sp.dma_start(st_c[m][0:DA], a_k[bass.ds(g, 1), 0].rearrange("g d t -> d g t")
                         .broadcast_to([DA, HH, T])).then_inc(s, 16)
            sp.dma_start(va[m][:, :, DA:2 * DA], a_v[bass.ds(g, 1)].rearrange("g p k d -> (g p) k d")).then_inc(s, 16)

        def a_sp(sp):
            for m in range(3):
                sp.dma_start(st_c[m][DA:DA + NSH], stack_const[24:24 + NSH].rearrange("p (h t) -> p h t", h=HH)) \
                    .then_inc(sem("a_sel"), 16)
            aload(sp, 0, 0)
            aload(sp, 1, 1)

            def body(g, m, o):
                if isinstance(g, int) and g + 2 >= NGA:
                    return
                if not (isinstance(g, int) and g == 0):
                    sp.wait_ge(sem("a_av"), UNITS * g)
                aload(sp, g + 2, (m + 2) % 3)

            run_groups(sp, NGA, body)
            sp.wait_ge(sem("a_sel"), 48)

        def a_pe(pe):
            def pass1(m, u, slot):
                h, i = u // TPC, u % TPC
                q = slice(i * P, (i + 1) * P)
                nc.tensor.matmul(score[slot], st_a[m][:, h, q], ka[m], start=True, stop=False)
                nc.tensor.matmul(score[slot], st_b[m][0:DA, h, q], st_c[m][0:DA, h, :], start=False,
                                 stop=True).then_inc(sem("a_s"), 1)

            def values(g, m, u, first):
                h, i = u // TPC, u % TPC
                pe.wait_ge(sem("a_exp"), UNITS * g + u + 1)
                if i == 0 and not (first and h < 2):
                    pe.wait_ge(sem("a_oset"), HH * g + h - 1)
                o = DA if h % 2 == 0 else 0
                nc.tensor.matmul(o_bank[h % 2], va[m][:, i, o:o + P], pbuf[:, u % 4, :], start=(i == 0),
                                 stop=(i == TPC - 1)).then_inc(sem("a_av"), 1)

            def turn_sums(g, pair):
                pe.wait_ge(sem("a_oset"), HH * g + 2 * pair + 2)
                for i in range(TPC):
                    for j in range(2):
                        last = nc.tensor.matmul(sh_bank[:, 2 * i + j:2 * i + j + 1], osum[:, j, i * P:(i + 1) * P],
                                                k("pick")[:, HH + j:HH + j + 1], start=True, stop=True)
                last.then_inc(sem("a_sums"), 1)

            def spread(g, pair):
                pe.wait_ge(sem("a_rec"), 2 * g + pair + 1)
                for i in range(TPC):
                    for j in range(2):
                        last = nc.tensor.matmul(sh_bank[DA * j:DA * j + DA, i * P:(i + 1) * P],
                                                rsum[:, 2 * i + j:2 * i + j + 1].broadcast_to([P, DA]), k("ident"),
                                                start=True, stop=True)
                last.then_inc(sem("a_spread"), 1)

            def project(g, m, pair, first):
                if pair == 0:
                    pe.wait_ge(sem("a_wset"), g + 1)
                    if not first:
                        pe.wait_ge(sem("a_add"), g)
                pe.wait_ge(sem("a_norm"), HH * g + 2 * pair + 2)
                nc.tensor.matmul(pr_bank, wog[:, m, pair * P:(pair + 1) * P], onorm[:, pair, :],
                                 start=(pair == 0), stop=(pair == 1)).then_inc(sem("a_pr"), 1)

            def turn_shift(g):
                pe.wait_ge(sem("a_shift"), g + 1)
                for i in range(TPC):
                    last = nc.tensor.matmul(sh_bank[0:NSH, i * P:(i + 1) * P], shift[:, i, :, :], identb[:, :],
                                            start=True, stop=True)
                last.then_inc(sem("a_turn"), 1)

            pe.wait_ge(sem("a_got0"), 80)
            for u in range(UNITS + LEAD_A):
                if u >= 2:
                    pe.wait_ge(sem("a_max"), u - 1)
                if u == UNITS:
                    turn_shift(0)
                    pe.wait_ge(sem("a_got1"), 80)
                pass1(u // UNITS, u % UNITS, u % 2)

            def body(g, m, o):
                first = isinstance(g, int) and g == 0
                if first:
                    pe.wait_ge(sem("a_sel"), 48)
                    pe.wait_ge(sem("a_ones"), 1)
                for u in range(UNITS):
                    h, i = u // TPC, u % TPC
                    ahead, u1 = 1 + (u + LEAD_A) // UNITS, (u + LEAD_A) % UNITS
                    if not (isinstance(g, int) and g + ahead >= NGA):
                        if u1 == 0:
                            pe.wait_ge(sem(f"a_got{(m + 2) % 3}"), 80 * (o + (m + 2) // 3 + 1))
                        pe.wait_ge(sem("a_max"), UNITS * (g + ahead) + u1 - 1)
                        pass1((m + ahead) % 3, u1, u1 % 2)
                    if i == 0:
                        pe.wait_ge(sem("a_shset"), HH * g + h + 1)
                    if not (first and u < 2):
                        pe.wait_ge(sem("a_exp"), UNITS * g + u - 1)
                    q = slice(i * P, (i + 1) * P)
                    nc.tensor.matmul(tscore[u % 2], ka[m][:, q], st_a[m][:, h, :], start=True, stop=False)
                    nc.tensor.matmul(tscore[u % 2], st_c[m][0:DA + NSH, h, q], st_b[m][0:DA + NSH, h, :],
                                     start=False, stop=True).then_inc(sem("a_t"), 1)
                    if u >= 1:
                        values(g, m, u - 1, first)
                    elif not first:
                        values(g - 1, (m + 2) % 3, UNITS - 1, False)
                    if not first and u == 3:
                        pe.wait_ge(sem("a_shset"), HH * g + HH)
                        turn_sums(g - 1, 1)
                    if not first and u == 5:
                        spread(g - 1, 1)
                    if not first and u == 7:
                        project(g - 1, (m + 2) % 3, 1, first)
                    if u == 11:
                        if first:
                            pe.wait_ge(sem("a_shset"), HH)
                        turn_sums(g, 0)
                    if u == 13:
                        spread(g, 0)
                    if u == 15:
                        project(g, m, 0, first)
                        if not (isinstance(g, int) and g == NGA - 1):
                            turn_shift(g + 1)

            run_groups(pe, NGA, body)
            values(NGA - 1, (NGA - 1) % 3, UNITS - 1, False)
            turn_sums(NGA - 1, 1)
            spread(NGA - 1, 1)
            project(NGA - 1, (NGA - 1) % 3, 1, False)

        def a_act(act):
            def shifts(g, m):
                act.wait_ge(sem("a_turn"), g + 1)
                for h in range(HH):
                    nc.scalar.activation(st_b[m][DA:DA + NSH, h, :], sh_bank[0:NSH, :], ACT.Copy) \
                        .then_inc(sem("a_shset"), 1)

            shifts(0, 0)

            def copy_out(g, h, first):
                act.wait_ge(sem("a_av"), UNITS * g + TPC * h + TPC)
                if not (first and h < 2):
                    act.wait_ge(sem("a_norm"), HH * g + h - 1)
                nc.scalar.activation(osum[:, h % 2, :], o_bank[h % 2], ACT.Copy).then_inc(sem("a_oset"), 1)

            def body(g, m, o):
                first = isinstance(g, int) and g == 0
                for u in range(UNITS):
                    act.wait_ge(sem("a_t"), UNITS * g + u + 1)
                    if not (first and u < 4):
                        act.wait_ge(sem("a_av"), UNITS * g + u - 3)
                    nc.scalar.activation(pbuf[:, u % 4, :], tscore[u % 2], ACT.Exp, scale=DA ** -0.5) \
                        .then_inc(sem("a_exp"), 1)
                    if u == 1 and not first:
                        copy_out(g - 1, 3, False)
                    if u == 7:
                        copy_out(g, 0, first)
                    if u == 9:
                        copy_out(g, 1, first)
                    if u == 14:
                        copy_out(g, 2, first)
                if not (isinstance(g, int) and g == NGA - 1):
                    shifts(g + 1, (m + 1) % 3)

            run_groups(act, NGA, body)
            copy_out(NGA - 1, 3, False)

        def a_dve(dve):
            def row_max(n, u):
                dve.wait_ge(sem("a_s"), n)
                h, i = u // TPC, u % TPC
                nc.vector.reduce_max(mx[:, i * HH + h:i * HH + h + 1], score[u % 2], AX.X).then_inc(sem("a_max"), 1)

            def negate(n, g):
                dve.wait_ge(sem("a_max"), n)
                m3 = mx[:, :].rearrange("p (i h) -> p i h", i=TPC)
                nc.vector.tensor_scalar(shift[:, :, 0, :], m3, -1.0, None, ALU.mult).then_inc(sem("a_shift_hi"), 1)
                dve.wait_ge(sem("a_shift_hi"), g + 1)
                nc.vector.scalar_tensor_tensor(shift[:, :, 1, :], m3, -1.0, shift[:, :, 0, :], ALU.mult,
                                               ALU.subtract).then_inc(sem("a_shift"), 1)
                dve.wait_ge(sem("a_shift"), g + 1)

            def add(g):
                dve.wait_ge(sem("a_pr"), 2 * g + 2)
                at = (g // HH) * T
                nc.vector.tensor_tensor(x[:, bass.ds(at, T)], x[:, bass.ds(at, T)], pr_bank, ALU.add) \
                    .then_inc(sem("a_add"), 1)

            def recip(g, pair):
                dve.wait_ge(sem("a_sums"), 2 * g + pair + 1)
                nc.vector.reciprocal(rsum[:, 0:2 * TPC], sh_bank[:, 0:2 * TPC]).then_inc(sem("a_rec"), 1)

            def norm(g, pair, first):
                dve.wait_ge(sem("a_spread"), 2 * g + pair + 1)
                if not first:
                    dve.wait_ge(sem("a_pr"), 2 * g + pair - 1)
                for j in range(2):
                    r = slice(DA * j, DA * j + DA)
                    nc.vector.tensor_tensor(onorm[r, pair, :], osum[r, j, :], sh_bank[r, :], ALU.mult) \
                        .then_inc(sem("a_norm"), 1)

            for u in range(UNITS + LEAD_A):
                if u == UNITS:
                    negate(UNITS, 0)
                row_max(u + 1, u % UNITS)

            def body(g, m, o):
                first = isinstance(g, int) and g == 0
                for u in range(UNITS):
                    ahead, u1 = 1 + (u + LEAD_A) // UNITS, (u + LEAD_A) % UNITS
                    if not (isinstance(g, int) and g + ahead >= NGA):
                        row_max(UNITS * (g + ahead) + u1 + 1, u1)
                        if u1 == UNITS - 1:
                            negate(UNITS * (g + 2), g + 1)
                    if not first and u == 4:
                        recip(g - 1, 1)
                    if not first and u == 6:
                        norm(g - 1, 1, isinstance(g, int) and g == 1)
                    if not first and u == 8:
                        add(g - 1)
                    if u == 12:
                        recip(g, 0)
                    if u == 14:
                        norm(g, 0, first)

            run_groups(dve, NGA, body)
            recip(NGA - 1, 1)
            norm(NGA - 1, 1, False)
            add(NGA - 1)

        def a_pool(pool):
            for m in range(3):
                nc.gpsimd.memset(va[m][:, :, 0:DA], 1.0)
                last = nc.gpsimd.memset(va[m][:, :, 2 * DA:3 * DA], 1.0)
            last.then_inc(sem("a_ones"), 1)

            def body(g, m, o):
                if not (isinstance(g, int) and g < 3):
                    pool.wait_ge(sem("a_pr"), 2 * g - 4)
                kv = g % HH
                nc.gpsimd.tensor_copy(wog[:, m, :], wsb[:, bass.ds(kv * (2 * P) + wofs["a_wpost"][0], 2 * P)]) \
                    .then_inc(sem("a_wset"), 1)

            run_groups(pool, NGA, body, 3, 0)

        class Narrow:
            def __init__(self, n, ln, tensors, groups_per_batch, heads, bias, masked, before):
                self.n, self.ln, self.tensors, self.gpb = n, ln, tensors, groups_per_batch
                self.heads, self.bias, self.masked = heads, bias, masked
                self.ng = B * groups_per_batch
                self.before = before
                self.pool_base = 4 * NPA * B if before is None else before.pool_base + 4 * before.np
                self.np = 2 * tensors * B

            def s(self, name):
                return sem(f"n_{name}")

            def base(self, name):
                if self.before is None:
                    return 0
                e = self.before
                if name[:3] == "got":
                    return 96 * len(range(int(name[3]), e.ng, 3))
                if name[:3] == "put":
                    return 32 * (e.np // 4)
                once = {"mask": 1, "maskput": 16, "rows": 96, "ones": 1, "vproj": NT, "vset": NT}
                if name in once:
                    return once[name]
                if name in ("proj", "full", "rest", "mid", "hi", "lo"):
                    return e.np
                return e.ng * {"s": UNITS, "max": UNITS, "t": UNITS, "exp": UNITS, "shset": HH, "av": TPC}.get(name, 1)

            def proj(self, idx):
                b, j = idx // (2 * self.tensors), idx % (2 * self.tensors)
                kind, tj = ("q", j) if j < self.tensors else ("k", j - self.tensors)
                return b, kind, tj

            def proj_pe(self, pe):
                ln_pe(pe, self.ln, x)
                for idx in range(self.np):
                    b, kind, tj = self.proj(idx)
                    pe.wait_ge(sem("ln_out"), B * self.ln + b + 1)
                    if idx == 4:
                        pe.wait_ge(sem("ln_out"), B * self.ln + B)
                    if idx >= 6:
                        pe.wait_ge(self.s("full"), self.base("full") + idx - 5)
                    nc.tensor.matmul(ps[:, idx % 6, :], w(f"{self.n}_w{kind}", tj * P, P), ch(xn, b), start=True,
                                     stop=True).then_inc(self.s("proj"), 1)
                for t in range(NT):
                    if t >= 2:
                        pe.wait_ge(self.s("vset"), self.base("vset") + t - 1)
                    nc.tensor.matmul(ps[:, 6 + t % 2, 0:C], xn[:, t * P:(t + 1) * P], w(f"{self.n}_wv"), start=True,
                                     stop=True).then_inc(self.s("vproj"), 1)

            def proj_act(self, act):
                ln_act(act, self.ln, xn)

                def middle(idx):
                    act.wait_ge(self.s("rest"), self.base("rest") + idx + 1)
                    nc.scalar.activation(parts_out[:, idx % 4, 1, :], ch(pb[1], idx % 4), ACT.Copy) \
                        .then_inc(self.s("mid"), 1)

                for idx in range(self.np):
                    act.wait_ge(self.s("proj"), self.base("proj") + idx + 1)
                    if idx >= 4:
                        act.wait_ge(self.s("rest"), self.base("rest") + idx - 3)
                    bias = v(self.bias[self.proj(idx)[1]])
                    nc.scalar.activation(ch(pb[0], idx % 4), ps[:, idx % 6, :], ACT.Identity, bias=bias) \
                        .then_inc(self.s("full"), 1)
                    if idx >= 1:
                        middle(idx - 1)
                middle(self.np - 1)

            def proj_dve(self, dve):
                ln_dve(dve, self.ln, x, xn)
                for idx in range(self.np):
                    dve.wait_ge(self.s("full"), self.base("full") + idx + 1)
                    if idx >= 4:
                        dve.wait_ge(self.s(f"put{idx % 4}"), self.base(f"put{idx % 4}") + 32 * (idx // 4))
                    nc.vector.tensor_copy(parts_out[:, idx % 4, 0, :], ch(pb[0], idx % 4)).then_inc(self.s("hi"), 1)
                    dve.wait_ge(self.s("hi"), self.base("hi") + idx + 1)
                    if idx >= 4:
                        dve.wait_ge(self.s("lo"), self.base("lo") + idx - 3)
                    nc.vector.tensor_tensor(ch(pb[1], idx % 4), ch(pb[0], idx % 4), parts_out[:, idx % 4, 0, :],
                                            ALU.subtract).then_inc(self.s("rest"), 1)
                for t in range(NT):
                    dve.wait_ge(self.s("vproj"), self.base("vproj") + t + 1)
                    src = ps[:, 6 + t % 2, 0:C]
                    if self.n == "c":
                        nc.vector.tensor_tensor(v_narrow[:, t, :], src, w("c_vb"), ALU.add).then_inc(self.s("vset"), 1)
                    else:
                        nc.vector.tensor_copy(v_narrow[:, t, :], src).then_inc(self.s("vset"), 1)
                if self.masked:
                    dve.wait_ge(sem("ln_out"), B * self.ln + B)
                    nc.vector.tensor_scalar(maskrow[0:1, :], xn[0:1, :], 0.0, -3e38, ALU.is_equal, ALU.mult) \
                        .then_inc(self.s("mask"), 1)
                else:
                    nc.vector.memset(maskrow[0:1, :], 0.0).then_inc(self.s("mask"), 1)
                    lam = w("lam").rearrange("p (a d) -> p a d", a=4)
                    link(dve, nc.vector.tensor_tensor(small[:, 0:2 * D8].rearrange("p (a d) -> p a d", a=2),
                                                      lam[:, 0:2, :], lam[:, 2:4, :], ALU.mult))
                    nc.vector.reduce_sum(small[:, 16:18], small[:, 0:2 * D8].rearrange("p (a d) -> p a d", a=2), AX.X) \
                        .then_inc(sem("lam_dot"), 1)
                    dve.wait_ge(sem("lam_exp"), 1)
                    link(dve, nc.vector.tensor_tensor(small[:, 20:21], small[:, 18:19], small[:, 19:20], ALU.subtract))
                    link(dve, nc.vector.tensor_scalar(small[:, 21:22], small[:, 20:21], LAMBDA_INIT + 1.0, -1.0,
                                                      ALU.add, ALU.mult))
                    link(dve, nc.vector.tensor_tensor(small[:, 22:23], small[:, 21:22], v("odd"), ALU.mult))
                    link(dve, nc.vector.tensor_scalar(small[:, 23:24], small[:, 22:23], 1.0, None, ALU.add))
                    nc.vector.tensor_scalar(w("b_wo"), w("b_wo"), small[:, 23:24], None, ALU.mult) \
                        .then_inc(sem("lam_set"), 1)

            def proj_sp(self, sp):
                for idx in range(self.np):
                    b, kind, tj = self.proj(idx)
                    dst = n_q if kind == "q" else n_k
                    g = self.gpb * b + HH * tj
                    for part, ready in ((0, "hi"), (1, "mid")):
                        sp.wait_ge(self.s(ready), self.base(ready) + idx + 1)
                        sp.dma_start(dst[g:g + 4, part].rearrange("g i h t -> g (i h) t"),
                                     parts_out[:, idx % 4, part, :]).then_inc(self.s(f"put{idx % 4}"), 16)
                sp.wait_ge(self.s("mask"), self.base("mask") + 1)
                sp.dma_start(n_mask.rearrange("b t -> (b t)").unsqueeze(0), maskrow[0:1, :]).then_inc(self.s("maskput"), 16)
                for m in range(3):
                    sp.dma_start(st_a[m][ROWS8:SHIFT8], stack_const[0:24].rearrange("p (h t) -> p h t", h=HH)) \
                        .then_inc(self.s("rows"), 16)
                    sp.dma_start(st_c[m][ROWS8 + 2:SHIFT8 + NSH], stack_const[2:32]
                                 .rearrange("p (h t) -> p h t", h=HH)).then_inc(self.s("rows"), 16)
                for i in range(4):
                    sp.wait_ge(self.s(f"put{i}"), self.base(f"put{i}") + 32 * self.np // 4)
                sp.wait_ge(self.s("maskput"), self.base("maskput") + 16)
                sp.wait_ge(self.s("rows"), self.base("rows") + 96)

            def proj_pool(self, pool):
                for m in range(3):
                    last = nc.gpsimd.memset(vn[m][:, :, :, :], 1.0)
                if not self.masked:
                    for c in range(B):
                        last = nc.gpsimd.memset(ch(acc_narrow, c), 0.0)
                last.then_inc(self.s("ones"), 1)
                for idx in range(self.np):
                    pool.wait_ge(self.s("mid"), self.base("mid") + idx + 1)
                    pool.wait_ge(sem(f"pool_put{idx % 4}"), self.pool_base + 16 * (idx // 4))
                    nc.gpsimd.tensor_tensor(parts_out[:, idx % 4, 2, :], ch(pb[1], idx % 4), parts_out[:, idx % 4, 1, :],
                                            ALU.subtract).then_inc(self.s("lo"), 1)
                    b, kind, tj = self.proj(idx)
                    dst = n_q if kind == "q" else n_k
                    g = self.gpb * b + HH * tj
                    pool.wait_ge(self.s("lo"), self.base("lo") + idx + 1)
                    pool.dma_start(dst[g:g + 4, 2].rearrange("g i h t -> g (i h) t"), parts_out[:, idx % 4, 2, :]) \
                        .then_inc(sem(f"pool_put{idx % 4}"), 16)
                for i in range(4):
                    pool.wait_ge(sem(f"pool_put{i}"), self.pool_base + 16 * self.np // 4)

            def load(self, sp, g, m):
                s = self.s(f"got{m}")
                for a in range(SPLIT8):
                    sp.dma_start(st_a[m][24 * a:24 * a + 24],
                                 n_q[bass.ds(g, 1), a].rearrange("g i h t -> g i (h t)").broadcast_to([3, D8, HH * T])) \
                        .then_inc(s, 16)
                sp.dma_start(st_c[m][0:ROWS8], n_k[bass.ds(g, 1)].rearrange("g a i h t -> g (a i) (h t)")
                             .broadcast_to([3, 24, HH * T])).then_inc(s, 16)
                b = g // self.gpb
                sp.dma_start(st_c[m][ROWS8:ROWS8 + 1], n_mask[bass.ds(b, 1)].unsqueeze(1).broadcast_to([1, HH, T])) \
                    .then_inc(s, 16)
                sp.dma_start(st_c[m][ROWS8 + 1:ROWS8 + 2], n_mask[bass.ds(b, 1)].unsqueeze(1)
                             .broadcast_to([1, HH, T])).then_inc(s, 16)

            def main_sp(self, sp):
                self.load(sp, 0, 0)
                self.load(sp, 1, 1)

                def body(g, m, o):
                    if isinstance(g, int) and g + 2 >= self.ng:
                        return
                    if not (isinstance(g, int) and g == 0):
                        sp.wait_ge(self.s("t"), self.base("t") + UNITS * g)
                    self.load(sp, g + 2, (m + 2) % 3)

                run_groups(sp, self.ng, body)

            def main_pe(self, pe):
                def pass1(m, u):
                    i, h = u // HH, u % HH
                    nc.tensor.matmul(n_score[(m + u) % 3], st_a[m][0:ROWS8 + 2, h, i * P:(i + 1) * P],
                                     st_c[m][0:ROWS8 + 2, h, :], start=True, stop=True).then_inc(self.s("s"), 1)

                def values(g, m, i, first):
                    pe.wait_ge(self.s("exp"), self.base("exp") + UNITS * g + HH * (i + 1))
                    if i == 0:
                        pe.wait_ge(self.s("vst"), self.base("vst") + g + 1)
                        if not first:
                            pe.wait_ge(self.s("oset"), self.base("oset") + g)
                    for h in range(HH):
                        last = nc.tensor.matmul(n_o[32 * h:32 * h + 32, :], vn[m][:, i, h, :],
                                                pbuf[:, HH * (i % 2) + h, :], start=(i == 0), stop=(i == TPC - 1))
                    last.then_inc(self.s("av"), 1)

                def turn_sums(g):
                    pe.wait_ge(self.s("oset"), self.base("oset") + g + 1)
                    if not (isinstance(g, int) and g == self.ng - 1):
                        pe.wait_ge(self.s("shset"), self.base("shset") + HH * g + 2 * HH)
                    else:
                        pe.wait_ge(self.s("add"), self.base("add") + g)
                    for i in range(TPC):
                        last = nc.tensor.matmul(n_x[:, HH * i:HH * i + HH], osum[:, 0, i * P:(i + 1) * P],
                                                k("pick")[:, 0:HH], start=True, stop=True)
                    last.then_inc(self.s("sums"), 1)

                def spread(g):
                    pe.wait_ge(self.s("rec"), self.base("rec") + g + 1)
                    for i in range(TPC):
                        for j in range(HH):
                            last = nc.tensor.matmul(n_x[32 * j:32 * j + 32, i * P:(i + 1) * P],
                                                    rsum[:, HH * i + j:HH * i + j + 1].broadcast_to([P, 32]),
                                                    k("ident"), start=True, stop=True)
                    last.then_inc(self.s("spread"), 1)

                def project(g, m):
                    pe.wait_ge(self.s("norm"), self.base("norm") + g + 1)
                    nc.tensor.matmul(n_x, wog[:, m, 0:P], onorm[:, 0, :], start=True, stop=True) \
                        .then_inc(self.s("pr"), 1)

                def turn_shift(g):
                    pe.wait_ge(self.s("shift"), self.base("shift") + g + 1)
                    for i in range(TPC):
                        last = nc.tensor.matmul(n_x[0:NSH, i * P:(i + 1) * P], shift[:, i, :, :], identb[:, :],
                                                start=True, stop=True)
                    last.then_inc(self.s("turn"), 1)

                pe.wait_ge(self.s("got0"), self.base("got0") + 96)
                for u in range(UNITS + LEAD_N):
                    if u >= 3:
                        pe.wait_ge(self.s("max"), self.base("max") + u - 2)
                    if u == UNITS:
                        turn_shift(0)
                        pe.wait_ge(self.s("got1"), self.base("got1") + 96)
                    pass1(u // UNITS, u % UNITS)

                def body(g, m, o):
                    first = isinstance(g, int) and g == 0
                    for u in range(UNITS):
                        i, h = u // HH, u % HH
                        ahead, u1 = 1 + (u + LEAD_N) // UNITS, (u + LEAD_N) % UNITS
                        if not (isinstance(g, int) and g + ahead >= self.ng):
                            if u1 == 0:
                                got = f"got{(m + 2) % 3}"
                                pe.wait_ge(self.s(got), self.base(got) + 96 * (o + (m + 2) // 3 + 1))
                            pe.wait_ge(self.s("max"), self.base("max") + UNITS * (g + ahead) + u1 - 2)
                            pass1((m + ahead) % 3, u1)
                        if i == 0:
                            pe.wait_ge(self.s("shset"), self.base("shset") + HH * g + h + 1)
                        if not (first and u < 3):
                            pe.wait_ge(self.s("exp"), self.base("exp") + UNITS * g + u - 2)
                        nc.tensor.matmul(n_tscore[(m + u) % 3], st_c[m][0:SHIFT8 + NSH, h, i * P:(i + 1) * P],
                                         st_a[m][0:SHIFT8 + NSH, h, :], start=True, stop=True).then_inc(self.s("t"), 1)
                        if u == 1 and not first:
                            values(g - 1, (m + 2) % 3, TPC - 1, False)
                        if h == 2 and i >= 1:
                            values(g, m, i - 1, first)
                        if u == 5 and not first:
                            turn_sums(g - 1)
                        if u == 7 and not first:
                            spread(g - 1)
                        if u == 10 and not first:
                            project(g - 1, (m + 2) % 3)
                        if u == 12 and not (isinstance(g, int) and g == self.ng - 1):
                            if not first:
                                pe.wait_ge(self.s("add"), self.base("add") + g)
                            turn_shift(g + 1)

                run_groups(pe, self.ng, body)
                values(self.ng - 1, (self.ng - 1) % 3, TPC - 1, False)
                turn_sums(self.ng - 1)
                spread(self.ng - 1)
                project(self.ng - 1, (self.ng - 1) % 3)

            def main_act(self, act):
                def shift_row(g, m, h):
                    act.wait_ge(self.s("turn"), self.base("turn") + g + 1)
                    nc.scalar.activation(st_a[m][SHIFT8:SHIFT8 + NSH, h, :], n_x[0:NSH, :], ACT.Copy) \
                        .then_inc(self.s("shset"), 1)

                for h in range(HH):
                    shift_row(0, 0, h)

                def copy_out(g, first):
                    act.wait_ge(self.s("av"), self.base("av") + TPC * g + TPC)
                    if not first:
                        act.wait_ge(self.s("norm"), self.base("norm") + g)
                    nc.scalar.activation(osum[:, 0, :], n_o, ACT.Copy).then_inc(self.s("oset"), 1)

                def body(g, m, o):
                    first = isinstance(g, int) and g == 0
                    for u in range(UNITS):
                        act.wait_ge(self.s("t"), self.base("t") + UNITS * g + u + 1)
                        if u % HH == 0 and not (first and u < 2 * HH):
                            act.wait_ge(self.s("av"), self.base("av") + TPC * g + u // HH - 1)
                        nc.scalar.activation(pbuf[:, u % 8, :], n_tscore[(m + u) % 3], ACT.Exp, scale=D8 ** -0.5) \
                            .then_inc(self.s("exp"), 1)
                        if u == 3 and not first:
                            copy_out(g - 1, isinstance(g, int) and g == 1)
                        if u >= 14 and not (isinstance(g, int) and g == self.ng - 1):
                            for h in (0, 1) if u == 14 else (2, 3):
                                shift_row(g + 1, (m + 1) % 3, h)

                run_groups(act, self.ng, body)
                copy_out(self.ng - 1, False)

            def main_dve(self, dve):
                def row_max(n, m, u):
                    dve.wait_ge(self.s("s"), self.base("s") + n)
                    nc.vector.reduce_max(mx[:, u:u + 1], n_score[(m + u) % 3], AX.X).then_inc(self.s("max"), 1)

                def negate(n, g):
                    dve.wait_ge(self.s("max"), self.base("max") + n)
                    m3 = mx[:, :].rearrange("p (i h) -> p i h", i=TPC)
                    nc.vector.tensor_scalar(shift[:, :, 0, :], m3, -1.0, None, ALU.mult).then_inc(self.s("shift_hi"), 1)
                    dve.wait_ge(self.s("shift_hi"), self.base("shift_hi") + g + 1)
                    nc.vector.scalar_tensor_tensor(shift[:, :, 1, :], m3, -1.0, shift[:, :, 0, :], ALU.mult,
                                                   ALU.subtract).then_inc(self.s("shift"), 1)
                    dve.wait_ge(self.s("shift"), self.base("shift") + g + 1)

                def recip(g):
                    dve.wait_ge(self.s("sums"), self.base("sums") + g + 1)
                    nc.vector.reciprocal(rsum[:, :], n_x[:, 0:UNITS]).then_inc(self.s("rec"), 1)

                def norm(g, first):
                    dve.wait_ge(self.s("spread"), self.base("spread") + g + 1)
                    if not first:
                        dve.wait_ge(self.s("pr"), self.base("pr") + g)
                    nc.vector.tensor_tensor(onorm[:, 0, :], osum[:, 0, :], n_x, ALU.mult) \
                        .then_inc(self.s("norm"), 1)

                def add(g):
                    dve.wait_ge(self.s("pr"), self.base("pr") + g + 1)
                    at = (g // self.gpb) * T
                    dst = x if self.masked else acc_narrow
                    nc.vector.tensor_tensor(dst[:, bass.ds(at, T)], dst[:, bass.ds(at, T)], n_x, ALU.add) \
                        .then_inc(self.s("add"), 1)

                for u in range(UNITS + LEAD_N):
                    if u == UNITS:
                        negate(UNITS, 0)
                    row_max(u + 1, u // UNITS, u % UNITS)

                def body(g, m, o):
                    first = isinstance(g, int) and g == 0
                    for u in range(UNITS):
                        ahead, u1 = 1 + (u + LEAD_N) // UNITS, (u + LEAD_N) % UNITS
                        if not (isinstance(g, int) and g + ahead >= self.ng):
                            row_max(UNITS * (g + ahead) + u1 + 1, (m + ahead) % 3, u1)
                            if u1 == UNITS - 1:
                                negate(UNITS * (g + 2), g + 1)
                        if u == 6 and not first:
                            recip(g - 1)
                        if u == 8 and not first:
                            norm(g - 1, isinstance(g, int) and g == 1)
                        if u == 11 and not first:
                            add(g - 1)

                run_groups(dve, self.ng, body)
                recip(self.ng - 1)
                norm(self.ng - 1, False)
                add(self.ng - 1)

            def main_pool(self, pool):
                def body(g, m, o):
                    b = g // self.gpb
                    gb = g % self.gpb
                    if not (isinstance(g, int) and g < 3):
                        pool.wait_ge(self.s("pr"), self.base("pr") + g - 2)
                    vt = ub[0]
                    if self.masked:
                        src = vt[:, bass.ds(b * T + gb * (HH * D8), (TPC - 1) * C + HH * D8)]
                        for i in range(TPC):
                            nc.gpsimd.tensor_copy(vn[m][:, i, :, 0:D8],
                                                  src[:, i * C:i * C + HH * D8].rearrange("p (h d) -> p h d", h=HH))
                    else:
                        src = vt[:, bass.ds(b * T + gb * (2 * D8), (TPC - 1) * C + 2 * D8)]
                        for i in range(TPC):
                            for s2 in range(2):
                                nc.gpsimd.tensor_copy(
                                    vn[m][:, i, :, 0:D8].rearrange("p (h s) d -> p h s d", s=2)[:, :, s2, :],
                                    src[:, i * C:i * C + 2 * D8].rearrange("p (h d) -> p h d", h=2))
                    nc.gpsimd.tensor_copy(wog[:, m, 0:P], wsb[:, bass.ds(gb * P + wofs[f"{self.n}_wo"][0], P)]) \
                        .then_inc(self.s("vst"), 1)

                run_groups(pool, self.ng, body, 3, 0)

        att_b = Narrow("b", 2, 2, 8, 2, {"q": "zero", "k": "zero"}, False, None)
        att_c = Narrow("c", 9, 1, 4, 4, {"q": "c_qb", "k": "c_kb"}, True, att_b)

        def bnorm_dve(dve):
            ln_dve(dve, 3, acc_narrow, pb[0], "b_gamma", "b_beta")
            for c in range(B):
                dve.wait_ge(sem("ln_out"), B * 3 + c + 1)
                nc.vector.tensor_tensor(ch(x, c), ch(x, c), ch(pb[0], c), ALU.add).then_inc(sem("bnorm_add"), 1)

        def mix_pe(pe, r, i):
            ln_pe(pe, i, x)
            for c in range(B):
                pe.wait_ge(sem("mix_r_in"), B * r + c + 1)
                nc.tensor.matmul(bankA[c], w("f_wr"), ch(tmp[0], c), start=True, stop=True).then_inc(sem("mix_r"), 1)
                pe.wait_ge(sem("mix_k_in"), B * r + c + 1)
                nc.tensor.matmul(bankB[c], w("f_wk"), ch(tmp[1], c), start=True, stop=True).then_inc(sem("mix_k"), 1)
            for c in range(B):
                pe.wait_ge(sem("mix_sq"), B * r + c + 1)
                nc.tensor.matmul(bankB[c], w("f_wv"), ch(tmp[3], c), start=True, stop=True).then_inc(sem("mix_v"), 1)

        def mix_act(act, r, i):
            ln_act(act, i, xn)
            for c in range(B):
                act.wait_ge(sem("mix_r"), B * r + c + 1)
                nc.scalar.activation(ch(tmp[2], c), bankA[c], ACT.Sigmoid).then_inc(sem("mix_sig"), 1)
                act.wait_ge(sem("mix_k"), B * r + c + 1)
                nc.scalar.activation(ch(tmp[3], c), bankB[c], ACT.Relu).then_inc(sem("mix_relu"), 1)
                act.wait_ge(sem("mix_relu"), B * r + c + 1)
                nc.scalar.activation(ch(tmp[3], c), ch(tmp[3], c), ACT.Square).then_inc(sem("mix_sq"), 1)

        def mix_dve(dve, r, i):
            ln_dve(dve, i, x, xn)
            for j, mu in enumerate(("f_mur", "f_muk")):
                link(dve, nc.vector.tensor_scalar(small[:, 24 + j:25 + j], v(mu), -1.0, 1.0, ALU.mult, ALU.add))
            for c in range(B):
                dve.wait_ge(sem("ln_out"), B * i + c + 1)
                for j, (mu, name) in enumerate((("f_mur", "mix_r_in"), ("f_muk", "mix_k_in"))):
                    d, s = ch(tmp[j], c), ch(xn, c)
                    link(dve, nc.vector.tensor_scalar(d, s, v(mu), None, ALU.mult))
                    nc.vector.scalar_tensor_tensor(d[:, 1:T], s[:, 0:T - 1], small[:, 24 + j:25 + j], d[:, 1:T],
                                                   ALU.mult, ALU.add).then_inc(sem(name), 1)
            for c in range(B):
                dve.wait_ge(sem("mix_v"), B * r + c + 1)
                dve.wait_ge(sem("mix_sig"), B * r + c + 1)
                link(dve, nc.vector.tensor_tensor(ch(tmp[2], c), ch(tmp[2], c), bankB[c], ALU.mult))
                nc.vector.tensor_tensor(ch(x, c), ch(x, c), ch(tmp[2], c), ALU.add).then_inc(sem("mix_add"), 1)

        X1, XN, XIL, GATE, XI, QF = tmp
        EQ, EK = ub
        KF = pb[0]
        TOK = pb[1]
        KT = [parts_out[:, 2 * j:2 * j + 2, :, :].rearrange("p a b t -> p (a b t)").bitcast(F32)[:, 0:T]
              for j in range(2)]
        mats = osum[:, 0, :]
        kvs = osum[:, 1, :]
        rkv = onorm[:, 0, :]

        def sub(t, c):
            return t[:, c * P:(c + 1) * P]

        def lin_pe(pe):
            ln_pe(pe, 5, x)
            ln_pe(pe, 6, X1, "l_x1")
            for c in range(B):
                pe.wait_ge(sem("ln_out"), B * 6 + c + 1)
                nc.tensor.matmul(bankA[c], w("m_in"), ch(XN, c), start=True, stop=True).then_inc(sem("l_in"), 1)
                nc.tensor.matmul(bankB[c], w("m_actp"), ch(XN, c), start=True, stop=True).then_inc(sem("l_actp"), 1)
            for c in range(B):
                pe.wait_ge(sem("l_xi"), c + 1)
                pe.wait_ge(sem("l_gate"), c + 1)
                nc.tensor.matmul(bankA[c], w("m_qk", 0, P), ch(XI, c), start=True, stop=True).then_inc(sem("l_q"), 1)
                nc.tensor.matmul(bankB[c], w("m_qk", P, P), ch(XI, c), start=True, stop=True).then_inc(sem("l_k"), 1)
            for c in range(B):
                pe.wait_ge(sem("l_km"), c + 1)
                nc.tensor.matmul(bankA[c], sub(mats, c), ch(QF, c), start=True, stop=True).then_inc(sem("l_den"), 1)
                for i in range(TPC):
                    last = nc.tensor.matmul(bankB[c][:, i * P:(i + 1) * P],
                                            KF[:, c * T + i * P:c * T + (i + 1) * P], k("ropeT"), start=True, stop=True)
                last.then_inc(sem("l_kt"), 1)
                pe.wait_ge(sem("l_ktset"), c + 1)
                for i in range(TPC):
                    last = nc.tensor.transpose(bankB[c][:, i * P:(i + 1) * P],
                                               XI[:, c * T + i * P:c * T + (i + 1) * P], k("ident"))
                last.then_inc(sem("l_vt"), 1)
                pe.wait_ge(sem("l_vtset"), c + 1)
                for i in range(TPC):
                    last = nc.tensor.matmul(bankB[c][:, 0:P], KT[c % 2][:, i * P:(i + 1) * P],
                                            TOK[:, c * T + i * P:c * T + (i + 1) * P], start=(i == 0),
                                            stop=(i == TPC - 1))
                last.then_inc(sem("l_kv"), 1)
            for c in range(B):
                pe.wait_ge(sem("l_kvset"), c + 1)
                nc.tensor.matmul(bankB[c][:, 0:P], k("rope"), sub(kvs, c), start=True, stop=True) \
                    .then_inc(sem("l_rkv"), 1)
            for c in range(B):
                pe.wait_ge(sem("l_rkvset"), c + 1)
                nc.tensor.matmul(bankB[c], sub(rkv, c), ch(QF, c), start=True, stop=True).then_inc(sem("l_num"), 1)
            for c in range(B):
                pe.wait_ge(sem("l_gated"), c + 1)
                nc.tensor.matmul(bankA[c], w("m_out"), ch(EQ, c), start=True, stop=True).then_inc(sem("l_out"), 1)
            ln_pe(pe, 7, X1, "l_x3")

            def fc2(n):
                c, f = n // FB, n % FB
                pe.wait_ge(sem("l_gelu"), n + 1)
                nc.tensor.matmul(bankB[c], w("m_fc2", f * P, P), pbuf[:, n % 8, :], start=(f == 0),
                                 stop=(f == FB - 1)).then_inc(sem("l_fc2"), 1)

            for n in range(B * FB):
                c, f = n // FB, n % FB
                if f == 0:
                    pe.wait_ge(sem("ln_out"), B * 7 + c + 1)
                if n >= 4:
                    pe.wait_ge(sem("l_gelu"), n - 3)
                nc.tensor.matmul(bankA[n % 4], w("m_fc1", f * P, P), ch(XN, c), start=True, stop=True) \
                    .then_inc(sem("l_fc1"), 1)
                if n >= 2:
                    fc2(n - 2)
            fc2(B * FB - 2)
            fc2(B * FB - 1)

        def lin_act(act):
            ln_act(act, 5, xn)
            ln_act(act, 6, XN)
            for c in range(B):
                act.wait_ge(sem("l_in"), c + 1)
                nc.scalar.activation(ch(XIL, c), bankA[c], ACT.Identity, bias=v("in_b")).then_inc(sem("l_xil"), 1)
            for c in range(B):
                act.wait_ge(sem("l_actp"), c + 1)
                nc.scalar.activation(ch(GATE, c), bankB[c], ACT.Silu, bias=v("actp_b")).then_inc(sem("l_gate"), 1)
            for c in range(B):
                act.wait_ge(sem("l_conv"), c + 1)
                nc.scalar.activation(ch(XI, c), ch(XI, c), ACT.Silu).then_inc(sem("l_xi"), 1)
            for c in range(B):
                act.wait_ge(sem("l_neg"), 2 * c + 1)
                nc.scalar.activation(ch(EQ, c), ch(EQ, c), ACT.Exp).then_inc(sem("l_exp"), 1)
                act.wait_ge(sem("l_neg"), 2 * c + 2)
                nc.scalar.activation(ch(EK, c), ch(EK, c), ACT.Exp).then_inc(sem("l_exp"), 1)
            for c in range(B):
                act.wait_ge(sem("l_kt"), c + 1)
                if c >= 2:
                    act.wait_ge(sem("l_kv"), c - 1)
                nc.scalar.activation(KT[c % 2], bankB[c], ACT.Copy).then_inc(sem("l_ktset"), 1)
                act.wait_ge(sem("l_vt"), c + 1)
                nc.scalar.activation(ch(TOK, c), bankB[c], ACT.Copy).then_inc(sem("l_vtset"), 1)
            for c in range(B):
                act.wait_ge(sem("l_den"), c + 1)
                nc.scalar.activation(ch(XIL, c), bankA[c], ACT.Identity, bias=v("tiny")).then_inc(sem("l_dn"), 1)
            ln_act(act, 7, XN)
            for n in range(B * FB):
                act.wait_ge(sem("l_fc1"), n + 1)
                if n >= 8:
                    act.wait_ge(sem("l_fc2"), n - 7)
                nc.scalar.activation(pbuf[:, n % 8, :], bankA[n % 4], ACT.Gelu, bias=v(f"fc1_b{n % FB}")) \
                    .then_inc(sem("l_gelu"), 1)

        def lin_dve(dve):
            ln_dve(dve, 5, x, xn)
            link(dve, nc.vector.tensor_scalar(v("cpe1_w1"), v("cpe1_w1"), 1.0, None, ALU.add))
            link(dve, nc.vector.tensor_scalar(v("cpe2_w1"), v("cpe2_w1"), 1.0, None, ALU.add))
            for c in range(B):
                dve.wait_ge(sem("ln_out"), B * 5 + c + 1)
                conv_dve(dve, X1, xn, c, "cpe1_w1", "cpe1_w0", "cpe1_w2", "cpe1_b").then_inc(sem("l_x1"), 1)
            dve.wait_ge(sem("l_x1"), B)
            ln_dve(dve, 6, X1, XN, "n1_g", "n1_b")
            for c in range(B):
                dve.wait_ge(sem("l_xil"), c + 1)
                conv_dve(dve, XI, XIL, c, "dwc_w1", "dwc_w0", "dwc_w2", "dwc_b").then_inc(sem("l_conv"), 1)
            for c in range(B):
                for bank, low, high, bias, ready in ((bankA[c], EQ, QF, "q_b", "l_q"), (bankB[c], EK, KF, "k_b", "l_k")):
                    dve.wait_ge(sem(ready), c + 1)
                    nc.vector.tensor_scalar(ch(low, c), bank, v(bias), 0.0, ALU.add, ALU.min).then_inc(sem("l_neg"), 1)
                    nc.vector.tensor_scalar(ch(high, c), bank, v(bias), 0.0, ALU.add, ALU.max) \
                        .then_inc(sem("l_pos"), 1)
            for c in range(B):
                dve.wait_ge(sem("l_pos"), 2 * c + 2)
                dve.wait_ge(sem("l_exp"), 2 * c + 2)
                nc.vector.tensor_tensor(ch(QF, c), ch(QF, c), ch(EQ, c), ALU.add)
                link(dve, nc.vector.tensor_tensor(ch(KF, c), ch(KF, c), ch(EK, c), ALU.add))
                link(dve, nc.vector.reduce_sum(small[:, 30 + c:31 + c], ch(KF, c), AX.X))
                nc.vector.tensor_scalar(sub(mats, c), k("block"), small[:, 30 + c:31 + c], 1.0 / T, ALU.mult,
                                        ALU.mult).then_inc(sem("l_km"), 1)
            for c in range(B):
                dve.wait_ge(sem("l_kv"), c + 1)
                nc.vector.scalar_tensor_tensor(sub(kvs, c), bankB[c][:, 0:P], 1.0 / T, k("block"), ALU.mult,
                                               ALU.mult).then_inc(sem("l_kvset"), 1)
            for c in range(B):
                dve.wait_ge(sem("l_rkv"), c + 1)
                nc.vector.tensor_copy(sub(rkv, c), bankB[c][:, 0:P]).then_inc(sem("l_rkvset"), 1)
            for c in range(B):
                link(dve, conv_dve(dve, EK, XI, c, "lepe_w1", "lepe_w0", "lepe_w2", "lepe_b"))
                dve.wait_ge(sem("l_dn"), c + 1)
                dve.wait_ge(sem("l_num"), c + 1)
                link(dve, nc.vector.reciprocal(ch(XIL, c), ch(XIL, c)))
                link(dve, nc.vector.tensor_tensor(ch(EQ, c), bankB[c], ch(XIL, c), ALU.mult))
                link(dve, nc.vector.tensor_tensor(ch(EQ, c), ch(EQ, c), ch(EK, c), ALU.add))
                nc.vector.tensor_tensor(ch(EQ, c), ch(EQ, c), ch(GATE, c), ALU.mult).then_inc(sem("l_gated"), 1)
            for c in range(B):
                dve.wait_ge(sem("l_out"), c + 1)
                link(dve, nc.vector.scalar_tensor_tensor(ch(EK, c), bankA[c], v("out_b"), ch(X1, c), ALU.add, ALU.add))
                conv_dve(dve, X1, EK, c, "cpe2_w1", "cpe2_w0", "cpe2_w2", "cpe2_b").then_inc(sem("l_x3"), 1)
            dve.wait_ge(sem("l_x3"), B)
            ln_dve(dve, 7, X1, XN, "n2_g", "n2_b")
            for c in range(B):
                dve.wait_ge(sem("l_fc2"), FB * (c + 1))
                link(dve, nc.vector.scalar_tensor_tensor(ch(X1, c), bankB[c], v("fc2_b"), ch(X1, c), ALU.add, ALU.add))
                nc.vector.tensor_tensor(ch(x, c), ch(x, c), ch(X1, c), ALU.add).then_inc(sem("l_add"), 1)

        route = std[:, 0:NT * 2 * NE]
        route3 = route.rearrange("p (t e) -> p t e", e=NE)
        route4 = route.rearrange("p (t s e) -> p t s e", s=2, e=NE)
        cw = std[:, 512:512 + NT * NE]
        cw3 = cw.rearrange("p (t e) -> p t e", e=NE)
        red = std[:, 768:768 + 2 * NT]
        cwc = std[:, 1024:1024 + TPC * NE]
        gate_sb = [ch(tmp[0], j) for j in range(4)]
        hid = [ch(tmp[1], j) for j in range(4)]
        xs = [ch(tmp[2], j) for j in range(2)]
        g_bank, u_bank = [ps[:, 0, :], ps[:, 1, :]], [ps[:, 2, :], ps[:, 3, :]]
        w_bank, y_bank = ps[:, 4, :], ps[:, 5, :]
        NU = NE * FB

        def moe_pe(pe, r, i):
            ln_pe(pe, i, x)
            if r == 0:
                pe.wait_ge(sem("moe_loaded"), 16)
            for t in range(NT):
                pe.wait_ge(sem("ln_out"), B * i + t // TPC + 1)
                last = nc.tensor.matmul(ps[:, 0, t * 2 * NE:(t + 1) * 2 * NE], xn[:, t * P:(t + 1) * P], w("e_route"),
                                        start=True, stop=True)
            last.then_inc(sem("e_logit"), 1)

            with pe.Fori(0, B) as c:
                cc = c + B * r

                def weights(e):
                    if e == 0:
                        pe.wait_ge(sem("e_cwc"), cc + 1)
                    else:
                        pe.wait_ge(sem("e_xs"), cc * NE + e)
                    for j in range(TPC):
                        last = nc.tensor.matmul(w_bank[:, j * P:(j + 1) * P],
                                                cwc[:, j * NE + e:j * NE + e + 1].broadcast_to([P, P]), k("ident"),
                                                start=True, stop=True)
                    last.then_inc(sem("e_w"), 1)

                def down(n):
                    e, f = n // FB, n % FB
                    pe.wait_ge(sem("e_hid"), cc * NU + n + 1)
                    nc.tensor.matmul(y_bank, moe[:, 2, e, f * P:(f + 1) * P], hid[n % 4], start=(n == 0),
                                     stop=(n == NU - 1)).then_inc(sem("e_down"), 1)

                weights(0)
                for n in range(NU):
                    e, f = n // FB, n % FB
                    if n >= 2:
                        pe.wait_ge(sem("e_hid"), cc * NU + n - 1)
                    nc.tensor.matmul(g_bank[n % 2], moe[:, 0, e, f * P:(f + 1) * P], xn[:, bass.ds(c * T, T)],
                                     start=True, stop=True).then_inc(sem("e_g"), 1)
                    if f == 0:
                        pe.wait_ge(sem("e_xs"), cc * NE + e + 1)
                    nc.tensor.matmul(u_bank[n % 2], moe[:, 1, e, f * P:(f + 1) * P], xs[e % 2], start=True,
                                     stop=True).then_inc(sem("e_u"), 1)
                    if n >= 1:
                        down(n - 1)
                    if f == 1 and e + 1 < NE:
                        weights(e + 1)
                down(NU - 1)

        def moe_act(act, r, i):
            ln_act(act, i, xn)
            for s2, scale in ((0, 1.0), (1, 10.0)):
                act.wait_ge(sem("e_cent"), r + 1)
                nc.scalar.activation(route4[:, :, s2, :], route4[:, :, s2, :], ACT.Exp, scale=scale) \
                    .then_inc(sem("e_rexp"), 1)
            with act.Fori(0, B) as c:
                cc = c + B * r
                for n in range(NU):
                    act.wait_ge(sem("e_g"), cc * NU + n + 1)
                    if n >= 4:
                        act.wait_ge(sem("e_hid"), cc * NU + n - 3)
                    nc.scalar.activation(gate_sb[n % 4], g_bank[n % 2], ACT.Silu).then_inc(sem("e_silu"), 1)

        def moe_dve(dve, r, i):
            ln_dve(dve, i, x, xn)
            dve.wait_ge(sem("e_logit"), r + 1)
            redb = red.unsqueeze(2).broadcast_to([P, 2 * NT, NE])
            link(dve, nc.vector.tensor_copy(route, ps[:, 0, 0:NT * 2 * NE]))
            link(dve, nc.vector.reduce_max(red, route3, AX.X))
            nc.vector.tensor_tensor(route3, route3, redb, ALU.subtract).then_inc(sem("e_cent"), 1)
            dve.wait_ge(sem("e_rexp"), 2 * r + 2)
            link(dve, nc.vector.reduce_sum(red, route3, AX.X))
            link(dve, nc.vector.reciprocal(red, red))
            link(dve, nc.vector.tensor_tensor(route3, route3, redb, ALU.mult))
            link(dve, nc.vector.tensor_tensor(cw3, route4[:, :, 0, :], route4[:, :, 1, :], ALU.mult))
            link(dve, nc.vector.reduce_sum(red[:, 0:NT], cw3, AX.X))
            link(dve, nc.vector.tensor_scalar(red[:, 0:NT], red[:, 0:NT], 1e-9, None, ALU.add))
            link(dve, nc.vector.reciprocal(red[:, 0:NT], red[:, 0:NT]))
            nc.vector.tensor_tensor(cw3, cw3, red[:, 0:NT].unsqueeze(2).broadcast_to([P, NT, NE]), ALU.mult).then_inc(sem("e_cw"), 1)
            dve.wait_ge(sem("e_cw"), r + 1)
            with dve.Fori(0, B) as c:
                cc = c + B * r
                at = bass.ds(c * T, T)
                nc.vector.tensor_copy(cwc, cw[:, bass.ds(c * (TPC * NE), TPC * NE)]).then_inc(sem("e_cwc"), 1)

                def scaled(e):
                    dve.wait_ge(sem("e_w"), cc * NE + e + 1)
                    nc.vector.tensor_tensor(xs[e % 2], xn[:, at], w_bank, ALU.mult).then_inc(sem("e_xs"), 1)

                scaled(0)
                for n in range(NU):
                    e, f = n // FB, n % FB
                    dve.wait_ge(sem("e_silu"), cc * NU + n + 1)
                    dve.wait_ge(sem("e_u"), cc * NU + n + 1)
                    if n >= 4:
                        dve.wait_ge(sem("e_down"), cc * NU + n - 3)
                    nc.vector.tensor_tensor(hid[n % 4], gate_sb[n % 4], u_bank[n % 2], ALU.mult) \
                        .then_inc(sem("e_hid"), 1)
                    if f == 1 and e + 1 < NE:
                        scaled(e + 1)
                dve.wait_ge(sem("e_down"), (cc + 1) * NU)
                nc.vector.tensor_tensor(x[:, at], x[:, at], y_bank, ALU.add).then_inc(sem("e_add"), 1)

        def out_pe(pe):
            for t in range(NT):
                nc.tensor.transpose(ps[:, t // TPC, (t % TPC) * P:(t % TPC + 1) * P], x[:, t * P:(t + 1) * P],
                                    k("ident")).then_inc(sem("y_turned"), 1)

        def out_act(act):
            for c in range(B):
                act.wait_ge(sem("y_turned"), TPC * (c + 1))
                nc.scalar.activation(ch(sq, c), bankA[c], ACT.Copy).then_inc(sem("y_set"), 1)

        def out_sp(sp):
            for c in range(B):
                sp.wait_ge(sem("y_set"), c + 1)
                sp.dma_start(out[c].rearrange("(t p) c -> p t c", p=P),
                             ch(sq, c).rearrange("p (t c) -> p t c", t=TPC)).then_inc(sem("y_out"), 16)
            sp.wait_ge(sem("y_out"), 16 * B)

        @block.sync
        def _(sp):
            load_sp(sp)
            stage_end(sp, 1)
            aproj_sp(sp)
            stage_end(sp, 2)
            a_sp(sp)
            stage_end(sp, 3)
            stage_end(sp, 4)
            att_b.proj_sp(sp)
            stage_end(sp, 5)
            att_b.main_sp(sp)
            stage_end(sp, 6)
            stage_end(sp, 7)
            stage_end(sp, 8)
            stage_end(sp, 9)
            stage_end(sp, 10)
            att_c.proj_sp(sp)
            stage_end(sp, 11)
            att_c.main_sp(sp)
            stage_end(sp, 12)
            stage_end(sp, 13)
            out_sp(sp)

        @block.gpsimd
        def _(pool):
            stage_end(pool, 1)
            aproj_pool(pool)
            stage_end(pool, 2)
            a_pool(pool)
            stage_end(pool, 3)
            stage_end(pool, 4)
            att_b.proj_pool(pool)
            stage_end(pool, 5)
            att_b.main_pool(pool)
            stage_end(pool, 6)
            stage_end(pool, 7)
            stage_end(pool, 8)
            stage_end(pool, 9)
            stage_end(pool, 10)
            att_c.proj_pool(pool)
            stage_end(pool, 11)
            att_c.main_pool(pool)
            stage_end(pool, 12)
            stage_end(pool, 13)

        @block.scalar
        def _(act):
            load_act(act)
            stage_end(act, 1)
            aproj_act(act)
            stage_end(act, 2)
            a_act(act)
            stage_end(act, 3)
            mix_act(act, 0, 1)
            stage_end(act, 4)
            att_b.proj_act(act)
            act.wait_ge(sem("lam_dot"), 1)
            nc.scalar.activation(small[:, 18:20], small[:, 16:18], ACT.Exp).then_inc(sem("lam_exp"), 1)
            stage_end(act, 5)
            att_b.main_act(act)
            stage_end(act, 6)
            ln_act(act, 3, pb[0])
            stage_end(act, 7)
            mix_act(act, 1, 4)
            stage_end(act, 8)
            lin_act(act)
            stage_end(act, 9)
            moe_act(act, 0, 8)
            stage_end(act, 10)
            att_c.proj_act(act)
            stage_end(act, 11)
            att_c.main_act(act)
            stage_end(act, 12)
            moe_act(act, 1, 10)
            stage_end(act, 13)
            out_act(act)

        @block.vector
        def _(dve):
            stage_end(dve, 1)
            aproj_dve(dve)
            stage_end(dve, 2)
            a_dve(dve)
            stage_end(dve, 3)
            mix_dve(dve, 0, 1)
            stage_end(dve, 4)
            att_b.proj_dve(dve)
            stage_end(dve, 5)
            att_b.main_dve(dve)
            stage_end(dve, 6)
            bnorm_dve(dve)
            stage_end(dve, 7)
            mix_dve(dve, 1, 4)
            stage_end(dve, 8)
            lin_dve(dve)
            stage_end(dve, 9)
            moe_dve(dve, 0, 8)
            stage_end(dve, 10)
            att_c.proj_dve(dve)
            stage_end(dve, 11)
            att_c.main_dve(dve)
            for c in range(B):
                dve.wait_ge(att_c.s("add"), att_c.base("add") + att_c.ng)
                nc.vector.tensor_scalar(ch(x, c), ch(x, c), v("c_ob"), None, ALU.add).then_inc(sem("c_bias"), 1)
            stage_end(dve, 12)
            moe_dve(dve, 1, 10)
            stage_end(dve, 13)

        @block.tensor
        def _(pe):
            load_pe(pe)
            stage_end(pe, 1)
            aproj_pe(pe)
            stage_end(pe, 2)
            a_pe(pe)
            stage_end(pe, 3)
            mix_pe(pe, 0, 1)
            stage_end(pe, 4)
            att_b.proj_pe(pe)
            stage_end(pe, 5)
            att_b.main_pe(pe)
            stage_end(pe, 6)
            ln_pe(pe, 3, acc_narrow)
            stage_end(pe, 7)
            mix_pe(pe, 1, 4)
            stage_end(pe, 8)
            lin_pe(pe)
            stage_end(pe, 9)
            moe_pe(pe, 0, 8)
            stage_end(pe, 10)
            att_c.proj_pe(pe)
            stage_end(pe, 11)
            att_c.main_pe(pe)
            stage_end(pe, 12)
            moe_pe(pe, 1, 10)
            stage_end(pe, 13)
            out_pe(pe)


def constants():
    eye = np.eye(P, dtype=np.float32)
    mean = np.full((P, P), 1.0 / C, np.float32)
    kk = np.arange(C // 2, dtype=np.float32)
    theta = (1.0 / np.float32(10000.0) ** (kk / np.float32(C // 2))).astype(np.float32)
    cos, sin = np.cos(theta).astype(np.float32), np.sin(theta).astype(np.float32)
    rope = np.zeros((C, C), np.float32)
    for i in range(C // 2):
        rope[2 * i, 2 * i], rope[2 * i, 2 * i + 1] = cos[i], -sin[i]
        rope[2 * i + 1, 2 * i], rope[2 * i + 1, 2 * i + 1] = sin[i], cos[i]
    head = np.arange(C) // D8
    same = (head[:, None] == head[None, :]).astype(np.float32)
    rows = np.arange(P)
    pick = (rows[:, None] == np.array([D8, 32 + D8, 64 + D8, 96 + D8, DA, 0])).astype(np.float32)
    cst = np.ascontiguousarray(np.concatenate([eye, mean, rope, rope.T, same, pick], axis=1))
    stack = np.zeros((32, HH, T), np.float32)
    stack[0:2] = 1.0
    for part in range(2):
        for h in range(HH):
            stack[24 + HH * part + h, h] = 1.0
    return cst, stack.reshape(32, HH * T), eye


def kernel(**inputs):
    import concourse.bacc as bacc
    from concourse.bass_utils import run_bass_kernel_spmd
    import ml_dtypes

    a = {n: np.asarray(t) for n, t in inputs.items()}
    cst, stack, eye = constants()

    def narrow(wt, tensors):
        return wt.reshape(C, tensors, 4, HH, D8).transpose(0, 1, 2, 4, 3).reshape(C, -1)

    def narrow_vec(b):
        return b.reshape(4, HH, D8).transpose(0, 2, 1).reshape(-1)

    def out_rows(wt, groups, per_head):
        o = np.zeros((P, groups, C), np.float32)
        for g in range(groups):
            for j in range(HH):
                hd = (HH * g + j) // per_head
                o[32 * j:32 * j + D8, g] = wt[hd * D8:(hd + 1) * D8]
        return o.reshape(P, -1)

    A, Bp, Fp, M, Cp, Ep = "L0_attn_a_", "L0_attn_b_", "L0_ffn_", "L1_attn_a_", "L1_attn_b_", "L1_ffn_"
    pack = {
        "a_wq": a[A + "Wq"], "a_wk": a[A + "Wk"], "a_wv": a[A + "Wv"],
        "a_wpost": a[A + "Wpost"].reshape(8, P, C).transpose(1, 0, 2).reshape(P, -1),
        "b_wq": narrow(a[Bp + "Wq"], 2), "b_wk": narrow(a[Bp + "Wk"], 2), "b_wv": a[Bp + "Wv"],
        "b_wo": out_rows(a[Bp + "Wo"], 8, 2),
        "c_wq": narrow(a[Cp + "wq_w"].T, 1), "c_wk": narrow(a[Cp + "wk_w"].T, 1), "c_wv": a[Cp + "wv_w"].T,
        "c_wo": out_rows(a[Cp + "wo_w"].T, 4, 1), "c_vb": np.broadcast_to(a[Cp + "wv_b"], (P, C)),
        "f_wr": a[Fp + "W_r"].T, "f_wk": a[Fp + "W_k"].T, "f_wv": a[Fp + "W_v"].T,
        "m_in": a[M + "in_w"], "m_actp": a[M + "actp_w"], "m_qk": a[M + "qk_w"], "m_out": a[M + "out_w"],
        "m_fc1": a[M + "fc1_w"], "m_fc2": a[M + "fc2_w"].reshape(FB, P, C).transpose(1, 0, 2).reshape(P, -1),
        "e_route": np.concatenate([a[Ep + "w_router"], a[Ep + "w_gating"]], axis=1),
        "lam": np.broadcast_to(np.concatenate([a[Bp + n] for n in ("lambda_q1", "lambda_q2", "lambda_k1",
                                                                   "lambda_k2")]), (P, 4 * D8)),
    }
    wts = np.ascontiguousarray(np.concatenate([pack[n] for n, _ in W_COLS], axis=1))
    vecs = {
        "f_mur": a[Fp + "mu_r"], "f_muk": a[Fp + "mu_k"], "c_qb": narrow_vec(a[Cp + "wq_b"]),
        "c_kb": narrow_vec(a[Cp + "wk_b"]), "c_ob": a[Cp + "wo_b"], "b_gamma": a[Bp + "gamma"],
        "b_beta": a[Bp + "beta"], "n1_g": a[M + "norm1_g"], "n1_b": a[M + "norm1_b"], "in_b": a[M + "in_b"],
        "actp_b": a[M + "actp_b"], "q_b": a[M + "qk_b"][:C], "k_b": a[M + "qk_b"][C:], "out_b": a[M + "out_b"],
        "n2_g": a[M + "norm2_g"], "n2_b": a[M + "norm2_b"], "fc2_b": a[M + "fc2_b"],
        "odd": ((np.arange(P) // 32) % 2).astype(np.float32), "zero": np.zeros(P, np.float32),
        "eps": np.full(P, EPS, np.float32), "tiny": np.full(P, 1e-6, np.float32),
    }
    for f in range(FB):
        vecs[f"fc1_b{f}"] = a[M + "fc1_b"][f * P:(f + 1) * P]
    for n in ("cpe1", "dwc", "lepe", "cpe2"):
        vecs[f"{n}_b"] = a[M + n + "_b"]
        for j in range(3):
            vecs[f"{n}_w{j}"] = a[M + n + "_w"][:, 0, j]
    vec = np.ascontiguousarray(np.stack([vecs[n] for n in V_COLS], axis=1))
    moe_w = np.ascontiguousarray(np.stack([
        a[Ep + "w_gate"].transpose(1, 0, 2), a[Ep + "w_up"].transpose(1, 0, 2),
        a[Ep + "w_down"].reshape(NE, FB, P, C).transpose(2, 0, 1, 3).reshape(P, NE, FF)], axis=1))
    arrays = {
        "x_in": np.ascontiguousarray(a[A + "X"]), "wts": wts, "cst": cst, "vec": vec, "moe_w": moe_w,
        "stack_const": stack.astype(ml_dtypes.bfloat16), "ident_bf": eye.astype(ml_dtypes.bfloat16),
    }
    nc = bacc.Bacc("TRN2", target_bir_lowering=False, num_devices=1)
    aps = [nc.dram_tensor(n, t.shape, mybir.dt.from_np(t.dtype), kind="ExternalInput").ap() for n, t in arrays.items()]
    out = nc.dram_tensor("out", (B, T, C), F32, kind="ExternalOutput").ap()
    build(nc, *aps, out)
    got = run_bass_kernel_spmd(nc, [arrays], core_ids=[0])
    return got.results[0]["out"]
```
